# Optimizing a Trainium2 kernel written in Bass

```python
import numpy as np
import jax
import jax.numpy as jnp

def _softmax(x, axis=-1):
    return jax.nn.softmax(x, axis=axis)

def _gelu(x):
    return jax.nn.gelu(x, approximate=True)

def _silu(x):
    return jax.nn.silu(x)

def _sigmoid(x):
    return jax.nn.sigmoid(x)

def _layernorm(x, axis=-1, eps=1e-05):
    m = jnp.mean(x, axis=axis, keepdims=True)
    v = jnp.var(x, axis=axis, keepdims=True)
    return (x - m) / jnp.sqrt(v + eps)

def _scatter_add(tgt, idx, src, axis=0):
    return tgt.at[idx].add(src)

def _segment_sum(src, seg, n):
    return jax.ops.segment_sum(src, seg, n)
kernel_name = 'mk_flamingo_gated_d1_seqx_r4_4ac406'

def setup_inputs(seed: int=0):
    np.random.seed(seed)
    _w = jnp.asarray

    def _rec_inputs():
        import jax
        import jax.numpy as jnp
        _rk = jax.random.key(seed)
        x = -0.0002928 + 1 * jax.random.normal(jax.random.fold_in(_rk, 1), (128, 128, 256), jnp.float32)
        _lenS = 128 - jax.random.randint(jax.random.fold_in(_rk, 7), (128,), 0, max(1, 128 // 4) + 1, jnp.int32)
        _lenS2 = 128 - jax.random.randint(jax.random.fold_in(_rk, 8), (128,), 0, max(1, 128 // 4) + 1, jnp.int32)
        _ctx_1024P = jax.random.normal(jax.random.fold_in(_rk, 11), (128, 16, 256), jnp.float32)
        _ctx_1024c = jax.random.dirichlet(jax.random.fold_in(_rk, 511), 0.3 * jnp.ones((16,), jnp.float32), (128, 128))
        _ctx_1024t = jnp.einsum('bsk,bkd->bsd', _ctx_1024c, _ctx_1024P)
        _ctx_1024t = _ctx_1024t * jax.lax.rsqrt(jnp.mean(jnp.square(_ctx_1024t)) + 1e-12) * 0.953939
        ctx_1024 = -1.39393e-06 + 0.999914 * (_ctx_1024t + 0.3 * jax.random.normal(jax.random.fold_in(_rk, 611), (128, 128, 256), jnp.float32))
        fside_Bx16xSxS2_0 = 9.80324e-05 + 1.00009 * jax.random.normal(jax.random.fold_in(_rk, 12), (128, 16, 128, 128), jnp.float32)
        _g = jax.random.normal(jax.random.fold_in(_rk, 9001), (2, 1), jnp.float32)
        _g = jnp.sign(_g) * jnp.maximum(jnp.abs(_g), 1.0) + (_g == 0) * 1.0
        g_xattn = _g[0]
        g_ffn = _g[1]
        return (x, ctx_1024, fside_Bx16xSxS2_0, g_xattn, g_ffn)
    x, ctx_1024, fside_Bx16xSxS2_0, g_xattn, g_ffn = _rec_inputs()

    def _L0_xattn_setup():
        import jax, jax.numpy as jnp
        import numpy as np
        HIDDEN = 256
        HEADS = 16
        D = HIDDEN // HEADS
        RANK = 8
        ALPHA = 16.0
        SCALING = ALPHA / RANK
        SCALE = D ** (-0.5)

        def _lora_proj(x, W, b, A, B):
            base = jnp.einsum('bsh,oh->bso', x, W) + b
            low = jnp.einsum('bsh,rh->bsr', x, A)
            return base + SCALING * jnp.einsum('bsr,or->bso', low, B)
        key = jax.random.key(seed)
        ks = jax.random.split(key, 20)
        Bt, S = (2, 512)
        inp = {'q': jax.random.normal(ks[0], (Bt, S, HIDDEN), dtype=jnp.float32), 'k': jax.random.normal(ks[1], (Bt, S, HIDDEN), dtype=jnp.float32), 'v': jax.random.normal(ks[2], (Bt, S, HIDDEN), dtype=jnp.float32), 'attn_bias': jax.random.normal(ks[3], (Bt, HEADS, S, S), dtype=jnp.float32)}
        sd = HIDDEN ** (-0.5)
        for i, name in enumerate(['q', 'k', 'v']):
            base = 4 + 4 * i
            inp[f'W{name}'] = jax.random.normal(ks[base + 0], (HIDDEN, HIDDEN), dtype=jnp.float32) * sd
            inp[f'b{name}'] = jnp.zeros((HIDDEN,), dtype=jnp.float32)
            inp[f'A{name}'] = jax.random.normal(ks[base + 1], (RANK, HIDDEN), dtype=jnp.float32) * sd
            inp[f'B{name}'] = jnp.zeros((HIDDEN, RANK), dtype=jnp.float32)
        return inp
    _L0_xattn_all = _L0_xattn_setup()
    _L0_xattn_in = {k: v for k, v in _L0_xattn_all.items() if k in ('Wq', 'bq', 'Aq', 'Bq', 'Wk', 'bk', 'Ak', 'Bk', 'Wv', 'bv', 'Av', 'Bv')}
    del _L0_xattn_all

    def _L0_ffn_setup():
        import jax, jax.numpy as jnp
        import numpy as np
        H = 256
        I = 256
        E = 8
        key = jax.random.key(seed)
        ks = jax.random.split(key, 8)
        s = 0.02
        x = jax.random.normal(ks[0], (4, 512, H), dtype=jnp.float32)
        Wg = jax.random.normal(ks[1], (H, E), dtype=jnp.float32) * s
        bg = jnp.zeros((E,), dtype=jnp.float32)
        W1 = jax.random.normal(ks[2], (E, H, I), dtype=jnp.float32) * s
        b1 = jnp.zeros((E, I), dtype=jnp.float32)
        W2 = jax.random.normal(ks[3], (E, I, H), dtype=jnp.float32) * s
        b2 = jnp.zeros((E, H), dtype=jnp.float32)
        return {'x': x, 'Wg': Wg, 'bg': bg, 'W1': W1, 'b1': b1, 'W2': W2, 'b2': b2}
    _L0_ffn_all = _L0_ffn_setup()
    _L0_ffn_in = {k: v for k, v in _L0_ffn_all.items() if k in ('Wg', 'bg', 'W1', 'b1', 'W2', 'b2')}
    del _L0_ffn_all
    return {'x': x, 'ctx_1024': ctx_1024, 'fside_Bx16xSxS2_0': fside_Bx16xSxS2_0, 'g_xattn': g_xattn, 'g_ffn': g_ffn, 'L0_xattn_Wq': _L0_xattn_in['Wq'], 'L0_xattn_bq': _L0_xattn_in['bq'], 'L0_xattn_Aq': _L0_xattn_in['Aq'], 'L0_xattn_Bq': _L0_xattn_in['Bq'], 'L0_xattn_Wk': _L0_xattn_in['Wk'], 'L0_xattn_bk': _L0_xattn_in['bk'], 'L0_xattn_Ak': _L0_xattn_in['Ak'], 'L0_xattn_Bk': _L0_xattn_in['Bk'], 'L0_xattn_Wv': _L0_xattn_in['Wv'], 'L0_xattn_bv': _L0_xattn_in['bv'], 'L0_xattn_Av': _L0_xattn_in['Av'], 'L0_xattn_Bv': _L0_xattn_in['Bv'], 'L0_ffn_Wg': _L0_ffn_in['Wg'], 'L0_ffn_bg': _L0_ffn_in['bg'], 'L0_ffn_W1': _L0_ffn_in['W1'], 'L0_ffn_b1': _L0_ffn_in['b1'], 'L0_ffn_W2': _L0_ffn_in['W2'], 'L0_ffn_b2': _L0_ffn_in['b2']}

def reference(x, ctx_1024, fside_Bx16xSxS2_0, g_xattn, g_ffn, L0_xattn_Wq, L0_xattn_bq, L0_xattn_Aq, L0_xattn_Bq, L0_xattn_Wk, L0_xattn_bk, L0_xattn_Ak, L0_xattn_Bk, L0_xattn_Wv, L0_xattn_bv, L0_xattn_Av, L0_xattn_Bv, L0_ffn_Wg, L0_ffn_bg, L0_ffn_W1, L0_ffn_b1, L0_ffn_W2, L0_ffn_b2):
    import jax
    import jax.numpy as jnp

    def _L0_xattn_ref(q, k, v, attn_bias, Wq, bq, Aq, Bq, Wk, bk, Ak, Bk, Wv, bv, Av, Bv):
        import jax, jax.numpy as jnp
        import numpy as np
        HIDDEN = 256
        HEADS = 16
        D = HIDDEN // HEADS
        RANK = 8
        ALPHA = 16.0
        SCALING = ALPHA / RANK
        SCALE = D ** (-0.5)

        def _lora_proj(x, W, b, A, B):
            base = jnp.einsum('bsh,oh->bso', x, W) + b
            low = jnp.einsum('bsh,rh->bsr', x, A)
            return base + SCALING * jnp.einsum('bsr,or->bso', low, B)
        Bt, S, _ = q.shape
        qh = _lora_proj(q, Wq, bq, Aq, Bq).reshape(Bt, S, HEADS, D)
        kh = _lora_proj(k, Wk, bk, Ak, Bk).reshape(Bt, S, HEADS, D)
        vh = _lora_proj(v, Wv, bv, Av, Bv).reshape(Bt, S, HEADS, D)
        scores = jnp.einsum('bqhd,bkhd->bhqk', qh * SCALE, kh) + attn_bias
        p = jax.nn.softmax(scores, axis=-1)
        out = jnp.einsum('bhqk,bkhd->bqhd', p, vh)
        return out.reshape(Bt, S, HEADS * D)

    def _L0_ffn_ref(x, Wg, bg, W1, b1, W2, b2):
        import jax, jax.numpy as jnp
        import numpy as np
        H = 256
        I = 256
        E = 8
        B, S, Hd = x.shape
        xf = x.reshape(-1, Hd)
        logits = xf @ Wg + bg
        gates = jax.nn.softmax(logits, axis=-1)
        idx = jnp.argmax(gates, axis=-1)
        h = jax.nn.gelu(jnp.einsum('th,ehi->tei', xf, W1) + b1, approximate=False)
        y = jnp.einsum('tei,eih->teh', h, W2) + b2
        out = jnp.take_along_axis(y, idx[:, None, None], axis=1)[:, 0, :]
        return out.reshape(B, S, Hd)
    x = x + jnp.tanh(g_xattn[0]) * _L0_xattn_ref(_layernorm(x, axis=-1), ctx_1024, ctx_1024, fside_Bx16xSxS2_0, L0_xattn_Wq, L0_xattn_bq, L0_xattn_Aq, L0_xattn_Bq, L0_xattn_Wk, L0_xattn_bk, L0_xattn_Ak, L0_xattn_Bk, L0_xattn_Wv, L0_xattn_bv, L0_xattn_Av, L0_xattn_Bv)
    x = x + jnp.tanh(g_ffn[0]) * _L0_ffn_ref(_layernorm(x, axis=-1), L0_ffn_Wg, L0_ffn_bg, L0_ffn_W1, L0_ffn_b1, L0_ffn_W2, L0_ffn_b2)
    return x

_drawn_inputs = setup_inputs


def setup_inputs(seed=0):
    import zlib

    import numpy as np

    out = dict(_drawn_inputs(seed))
    spreads = {'L0_xattn_bq': (0.0, 0.1),
     'L0_xattn_Bq': (0.0, 0.1),
     'L0_xattn_bk': (0.0, 0.8),
     'L0_xattn_Bk': (0.0, 0.1),
     'L0_xattn_bv': (0.0, 0.1),
     'L0_xattn_Bv': (0.0, 0.1),
     'L0_ffn_bg': (0.0, 0.1),
     'L0_ffn_b1': (0.0, 0.539),
     'L0_ffn_b2': (0.0, 0.1)}
    factors = {}
    for name, (base, spread) in spreads.items():
        noise = np.random.default_rng([zlib.crc32(name.encode()), seed]).standard_normal(out[name].shape)
        drawn = base * np.exp(spread * noise) if base else spread * noise
        out[name] = jnp.asarray(drawn.astype(out[name].dtype))
    for name, factor in factors.items():
        out[name] = (out[name] * factor).astype(out[name].dtype)
    return out
```

```python
from contextlib import ExitStack

import concourse.bass as bass
from concourse import mybir

F32 = mybir.dt.float32
I32 = mybir.dt.int32
BF16 = mybir.dt.bfloat16
ALU = mybir.AluOpType
ACT = mybir.ActivationFunctionType
AX = mybir.AxisListType

P = 128
N = 128
HID = 256
KC = HID // P
HEADS = 16
D = HID // HEADS
RANK = 8
LORA = 16.0 / RANK
EXPERTS = 8
EPS = 1e-5
TOKENS = N * P
U = 8

FT = 256
HALVES = FT // P
TILES = 72
FU = 8
NO_TOKEN = 1 << 20
LIST = EXPERTS * TOKENS + TILES * FT

PAIRS = [(0, 0), (0, 1), (0, 2), (1, 0), (1, 1), (2, 0)]
ROWS = D * len(PAIRS)

C_ID, C_TRI, C_ONE, C_IOTA, C_BASE = 0, 128, 256, 384, 416
C_HALF = 448
C_END = 449
R_M, R_J, R_J256 = 0, EXPERTS * (TOKENS // FT), EXPERTS * (TOKENS // FT) + TILES * EXPERTS
R_END = R_J256 + TILES


class At:

    def __init__(self, i, k, width):
        self.i, self.k, self.width = i, k, width

    def slot(self, m):
        return self.k % m

    def n(self, mul=1, add=0):
        v = self.k * mul + add
        return self.i * (self.width * mul) + v

    def per(self, m, mul=1, add=0):
        v = (self.k // m) * mul + add
        return self.i * (self.width // m * mul) + v

    def minus(self, lag):
        return At(self.i, self.k - lag, self.width)

    def reached(self, least):
        return not isinstance(self.i, int) or self.i * self.width + self.k >= least


def run_steps(eng, first, last, width, loop_rounds, body):
    a, b = loop_rounds
    for s in range(first, a * width):
        body(0, s)
    with eng.Fori(a, b) as i:
        for k in range(width):
            body(i, k)
    for s in range(b * width, last + 1):
        body(0, s)


def flamingo_block(nc, x, ctx_in, bias, g_xattn, g_ffn, wqT, bq, aq, bqT, wkT, bk, ak, bkT, wvT, bv, av, bvT,
                   wg, bg, w1, b1, w2, b2, consts, row_consts, ids_const, out):
    ctx = ExitStack()
    with ctx:
        def sb(name, shape, dt=F32):
            return ctx.enter_context(nc.sbuf_tensor(name, shape, dt))

        def sem(name):
            return ctx.enter_context(nc.semaphore(name))

        x2_dram = nc.dram_tensor("x2_dram", (TOKENS, HID), F32, kind="Internal").ap()
        list_dram = nc.dram_tensor("list_dram", (LIST, 1), I32, kind="Internal").ap()

        cst = sb("cst", [P, C_END])
        row = sb("row", [1, R_END])
        ids4 = sb("ids4", [P, 4])
        ids4_i = sb("ids4_i", [P, 4], I32)
        empty = sb("empty", [P, LIST // P], I32)
        ident, tri, ones = cst[:, C_ID:C_ID + P], cst[:, C_TRI:C_TRI + P], cst[:, C_ONE:C_ONE + P]
        minus_half = cst[:, C_HALF:C_HALF + 1]
        iota = cst[:, C_IOTA:C_IOTA + 32].rearrange("p (j e) -> p j e", e=EXPERTS)
        ebase = cst[:, C_BASE:C_BASE + 32].rearrange("p (j e) -> p j e", e=EXPERTS)
        W = {w: sb(f"w{w}", [P, KC, HID]) for w in "qkv"}
        A = {w: sb(f"a{w}", [RANK, HID]) for w in "qkv"}
        B = {w: sb(f"b{w}", [RANK, HID]) for w in "qkv"}
        bq_col = sb("bq_col", [P, KC])
        bk_col = sb("bk_col", [P, KC])
        bv_all = sb("bv_all", [P, HID])
        bg_all = sb("bg_all", [P, EXPERTS])
        wg_sb = sb("wg_sb", [P, KC, EXPERTS])
        g_raw = sb("g_raw", [P, 2])
        tg = sb("tg", [P, 2])

        x_sb = sb("x_sb", [P, 4, HID])
        xr = sb("xr", [P, 8, HID])
        ctx_sb = sb("ctx_sb", [P, 4, HID])
        sc = sb("sc", [P, 4, HEADS * P])
        xn = sb("xn", [P, 2, HID])
        XT = sb("XT", [P, 2, 2 * KC, 2 * P])
        F = {w: sb(f"f{w}", [P, KC * 2 * P]) for w in "qk"}
        REST = {w: sb(f"rest{w}", [P, KC * 2 * P]) for w in "qk"}
        PART = {w: sb(f"part{w}", [P, 3, KC * 2 * P], BF16) for w in "qk"}
        ST = {w: sb(f"st{w}", [ROWS, 2, HEADS, 2 * P], BF16) for w in "qk"}
        V = sb("V", [P, 8, HEADS, D + 1])
        PT = sb("PT", [P, HEADS * P])
        negmax = sb("negmax", [P, 2, HEADS])
        rden = sb("rden", [P, HEADS])
        x2 = sb("x2", [P, 2, HID])
        xn2 = sb("xn2", [P, 2, HID])
        x2T = sb("x2T", [P, 2, KC, P])
        st1, mv1, ve1, rs1 = sb("st1", [P, 6]), sb("mv1", [P, 2]), sb("ve1", [P, 1]), sb("rs1", [P, 1])
        st2, mv2, ve2, rs2 = sb("st2", [P, 6]), sb("mv2", [P, 2]), sb("ve2", [P, 1]), sb("rs2", [P, 1])
        L = sb("L", [P, 4, EXPERTS])
        lmax, key, pick = sb("lmax", [P, 4]), sb("key", [P, 4, EXPERTS]), sb("pick", [P, 4])
        OH = sb("OH", [P, 4, EXPERTS])
        CNT = sb("CNT", [P, 5, EXPERTS])
        where = sb("where", [P, 4, EXPERTS])
        slot_f = sb("slot_f", [P, 4])
        slot_i = sb("slot_i", [P, 4], I32)

        cnt = sb("cnt", [1, EXPERTS])
        over = sb("over", [1, EXPERTS, TOKENS // FT])
        nt = sb("nt", [1, EXPERTS])
        zero8 = sb("zero8", [1, EXPERTS])
        end = sb("end", [1, EXPERTS])
        past = sb("past", [1, TILES, EXPERTS])
        ptn = sb("ptn", [1, TILES, EXPERTS])
        e_f, s_f, b_f, ec_f = (sb(t, [1, TILES]) for t in ("e_f", "s_f", "b_f", "ec_f"))
        tile_e = sb("tile_e", [1, TILES], I32)
        tile_b = sb("tile_b", [1, TILES], I32)
        ids = sb("ids", [P, 8, HALVES], I32)
        idc = sb("idc", [P, 4, HALVES], I32)
        xg = sb("xg", [P, 4, HALVES, HID])
        xgn = sb("xgn", [P, 2, HALVES, HID])
        xgT = sb("xgT", [P, 2, KC, FT])
        hT = sb("hT", [P, 2, KC, FT])
        w1_sb = sb("w1_sb", [P, 2, KC, HID])
        b1_sb = sb("b1_sb", [P, 2, KC])
        w2_sb = sb("w2_sb", [P, 4, KC, HID])
        b2_sb = sb("b2_sb", [P, 4, HID])
        stg, mvg = sb("stg", [P, HALVES, 6]), sb("mvg", [P, HALVES, 2])
        veg, rsg = sb("veg", [P, HALVES]), sb("rsg", [P, HALVES])
        yb = sb("yb", [P, HALVES, HID])
        og = sb("og", [P, 2, HALVES, HID])

        bank = [ctx.enter_context(nc.psum_tensor(f"bank{i}", [P, 512], F32)) for i in range(8)]
        b_s, b_t = bank[0:2], bank[2:4]
        b_o, b_x, b_vk, b_q = bank[4], bank[5], bank[6], bank[7]
        o_ps = b_o[:, 0:HEADS * (D + 1)].rearrange("p (h d) -> p h d", d=D + 1)
        log_ps = b_o[:, 288:288 + EXPERTS]
        pos_ps = b_o[:, 320:352].rearrange("p (j e) -> p j e", e=EXPERTS)

        s_set = sem("s_set")
        s_list0 = sem("s_list0")
        s_setp, s_setd, s_seta, s_setg = sem("s_setp"), sem("s_setd"), sem("s_seta"), sem("s_setg")
        x_in = [sem(f"x_in{i}") for i in range(4)]
        ctx_inn = [sem(f"ctx_in{i}") for i in range(4)]
        bias_in = [sem(f"bias_in{i}") for i in range(4)]
        st1_ok, mv1_ok, ve1_ok, rs1_ok, xn_ok = (sem(t) for t in ("st1_ok", "mv1_ok", "ve1_ok", "rs1_ok", "xn_ok"))
        xt_ready, xt_evac = sem("xt_ready"), sem("xt_evac")
        v_ready, v_evac = sem("v_ready"), sem("v_evac")
        q_ready, q_evac, k_ready, k_evac = sem("q_ready"), sem("q_evac"), sem("k_ready"), sem("k_evac")
        p0_ok, p1_ok, rest_ok, p2_ok = sem("p0_ok"), sem("p1_ok"), sem("rest_ok"), sem("p2_ok")
        qk_in = [sem(f"qk_in{i}") for i in range(2)]
        s_ready, s_used, max_ok, sub_ok = sem("s_ready"), sem("s_used"), sem("max_ok"), sem("sub_ok")
        tr_ready, pt_ready = sem("tr_ready"), sem("pt_ready")
        o_ready, o_used = sem("o_ready"), sem("o_used")
        rden_ok, xr_ok, x2_ok = sem("rden_ok"), sem("xr_ok"), sem("x2_ok")
        x2_out = [sem(f"x2_out{i}") for i in range(2)]
        st2_ok, mv2_ok, ve2_ok, rs2_ok, xn2_ok = (sem(t) for t in ("st2_ok", "mv2_ok", "ve2_ok", "rs2_ok", "xn2_ok"))
        x2t_ready, x2t_evac = sem("x2t_ready"), sem("x2t_evac")
        l_ok, lmax_ok, lt_ok, key_ok, pick_ok, oh_ok, cnt0_ok, cnt_ok = (
            sem(t) for t in ("l_ok", "lmax_ok", "lt_ok", "key_ok", "pick_ok", "oh_ok", "cnt0_ok", "cnt_ok"))
        ids4_ok, ids4_next = sem("ids4_ok"), sem("ids4_next")
        pos_ok, where_ok, slotf_ok, slot_ok, ids_out = (
            sem(t) for t in ("pos_ok", "where_ok", "slotf_ok", "slot_ok", "ids_out"))
        c_ready, s_tab, tab_ok = sem("c_ready"), sem("s_tab"), sem("tab_ok")
        ids_in = [sem(f"ids_in{i}") for i in range(8)]
        w1_in = [sem(f"w1_in{i}") for i in range(2)]
        w2_in = [sem(f"w2_in{i}") for i in range(4)]
        idc_ok = sem("idc_ok")
        xg_in = [sem(f"xg_in{i}") for i in range(4)]
        stg_ok, mvg_ok, veg_ok, rsg_ok, xgn_ok = (sem(t) for t in ("stg_ok", "mvg_ok", "veg_ok", "rsg_ok", "xgn_ok"))
        gt_ready, gt_evac, h_ready, h_ok, y_ready, y_used, og_ok = (
            sem(t) for t in ("gt_ready", "gt_evac", "h_ready", "h_ok", "y_ready", "y_used", "og_ok"))
        og_out = [sem(f"og_out{i}") for i in range(2)]

        SETUP_DMAS = 20
        x_seq = x.rearrange("(a n) s h -> n s (a h)", a=1)
        ctx_seq = ctx_in.rearrange("(a n) s h -> n s (a h)", a=1)
        bias_seq = bias.rearrange("n h q k -> n q h k")
        x2_seq = x2_dram.rearrange("(n s) h -> n s h", s=P)
        out_rows = out.rearrange("n s h -> (n s) h")

        LOOP = (1, N // U - 1)
        FIRST, LAST = -6, N + 5
        FLOOP = (1, TILES // FU - 1)
        FFIRST, FLAST = -4, TILES + 2

        block = ctx.enter_context(nc.Block())

        def seq(i, k, lag):
            t = At(i, k - lag, U)
            if isinstance(i, int) and not 0 <= i * U + k - lag < N:
                return None
            return t

        def tile(i, k, lag):
            t = At(i, k - lag, FU)
            if isinstance(i, int) and not 0 <= i * FU + k - lag < TILES:
                return None
            return t

        @block.sync
        def _(sp):
            def load(dst, src):
                sp.dma_start(dst, src).then_inc(s_set, 16)

            load(cst[:], consts)
            load(row[:], row_consts)
            load(ids4[:], ids_const)
            for w, wt, a, b in (("q", wqT, aq, bqT), ("k", wkT, ak, bkT), ("v", wvT, av, bvT)):
                load(W[w][:], wt)
                load(A[w][:], a)
                load(B[w][:], b)
            load(bq_col[:], bq)
            load(bk_col[:], bk)
            load(bv_all[:], bv.partition_broadcast(P))
            load(bg_all[:], bg.partition_broadcast(P))
            load(wg_sb[:], wg)
            load(g_raw[:, 0:1], g_xattn.partition_broadcast(P))
            load(g_raw[:, 1:2], g_ffn.partition_broadcast(P))
            load(cnt[:], bg)
            sp.wait_ge(s_setg, 1)
            sp.dma_start(list_dram.rearrange("(p c) o -> p (c o)", p=P), empty[:]).then_inc(s_list0, 16)

            def step(i, k):
                t = seq(i, k, -6)
                if t:
                    if t.reached(4):
                        sp.wait_ge(xr_ok, t.n(1, -3))
                        sp.nop(nofuse=True)
                        sp.wait_ge(xn_ok, t.n(1, -3))
                        sp.nop(nofuse=True)
                        sp.wait_ge(xt_ready, t.n(1, -3))
                        sp.nop(nofuse=True)
                    sp.dma_start(x_sb[:, t.slot(4), :], x_seq[t.n()]).then_inc(x_in[t.slot(4)], 16)
                    sp.dma_start(ctx_sb[:, t.slot(4), :], ctx_seq[t.n()]).then_inc(ctx_inn[t.slot(4)], 16)
                t = seq(i, k, -2)
                if t and t.slot(2) == 0:
                    pair = t.k // 2 % 2
                    sp.wait_ge(p2_ok, t.per(2, 2, 2))
                    sp.nop(nofuse=True)
                    if t.reached(4):
                        sp.wait_ge(s_ready, t.n(4, -8))
                    sp.nop(nofuse=True)
                    for w, which in (("q", 0), ("k", 1)):
                        for r, parts in enumerate(PAIRS):
                            sp.dma_start(ST[w][D * r:D * r + D, pair].rearrange("d (h c) t -> d h (c t)", c=KC),
                                         PART[w][:, parts[which], :]).then_inc(qk_in[pair], 16)
                t = seq(i, k, 2)
                if t:
                    sp.wait_ge(x2_ok, t.n(1, 1))
                    sp.nop(nofuse=True)
                    sp.dma_start(x2_seq[t.n()], x2[:, t.slot(2), :]).then_inc(x2_out[t.slot(2)], 16)
                t = seq(i, k, -3)
                if t:
                    if t.reached(4):
                        sp.wait_ge(tr_ready, t.n(4, -12))
                        sp.nop(nofuse=True)
                    for h in range(0, HEADS, 8):
                        sp.dma_start(sc[:, t.slot(4), h * P:(h + 8) * P].rearrange("p (h k) -> p h k", h=8),
                                     bias_seq[t.n(), :, h:h + 8, :]).then_inc(bias_in[t.slot(4)], 16)

            run_steps(sp, FIRST, LAST, U, LOOP, step)

            for q in x2_out:
                sp.wait_ge(q, 16 * (N // 2))
            sp.wait_ge(ids_out, 16 * N)
            sp.wait_ge(tab_ok, 1)

            def fstep(i, k):
                t = tile(i, k, -3)
                if t:
                    if t.reached(8):
                        sp.wait_ge(og_out[t.slot(2)], t.per(2, 16 * HALVES, -48 * HALVES))
                        sp.nop(nofuse=True)
                    b = sp.value_load(tile_b[0:1, bass.ds(t.n(), 1)], min_val=0, max_val=LIST - FT)
                    sp.dma_start(ids[:, t.slot(8), :],
                                 list_dram[bass.ds(b, FT), :].rearrange("(p a) o -> p (a o)", p=P)
                                 ).then_inc(ids_in[t.slot(8)], 16)
                t = tile(i, k, -1)
                if t:
                    if t.reached(2):
                        sp.wait_ge(h_ok, t.n(1, -1))
                        sp.nop(nofuse=True)
                    if t.reached(4):
                        sp.wait_ge(og_ok, t.n(1, -3))
                        sp.nop(nofuse=True)
                    e = sp.value_load(tile_e[0:1, bass.ds(t.n(), 1)], min_val=0, max_val=EXPERTS - 1)
                    sp.dma_start(w1_sb[:, t.slot(2)], w1[e]).then_inc(w1_in[t.slot(2)], 16)
                    sp.dma_start(b1_sb[:, t.slot(2)], b1[e]).then_inc(w1_in[t.slot(2)], 16)
                    sp.dma_start(w2_sb[:, t.slot(4)], w2[e]).then_inc(w2_in[t.slot(4)], 16)
                    sp.dma_start(b2_sb[:, t.slot(4)], b2[bass.ds(e, 1), :].partition_broadcast(P).rearrange(
                        "p a h -> p (a h)")).then_inc(w2_in[t.slot(4)], 16)

            run_steps(sp, FFIRST, FLAST, FU, FLOOP, fstep)
            for q in og_out:
                sp.wait_ge(q, 16 * HALVES * TILES // 2)

        @block.gpsimd
        def _(pool):
            nc.gpsimd.memset(empty[:], NO_TOKEN).then_inc(s_setg, 1)
            nc.gpsimd.memset(V[:], 1.0).then_inc(s_setg, 1)
            pool.wait_ge(s_setd, 9)
            pool.wait_ge(s_list0, 16)

            def step(i, k):
                t = seq(i, k, -5)
                if t:
                    pool.wait_ge(ve1_ok, t.n(1, 1))
                    nc.gpsimd.tensor_tensor(rs1[:], ve1[:], minus_half, ALU.pow).then_inc(rs1_ok, 1)
                    if t.reached(8):
                        pool.wait_ge(x2_ok, t.n(1, -7))
                    nc.gpsimd.tensor_tensor(xr[:, t.slot(8), :], x_sb[:, t.slot(4), :], bv_all[:],
                                            ALU.add).then_inc(xr_ok, 1)
                t, done = seq(i, k, 0), seq(i, k, 2)
                late, proj = seq(i, k, -2), seq(i, k, -4)
                for h in range(2):
                    if h and late and late.slot(2) == 0:
                        for n, w in enumerate("qk"):
                            pool.wait_ge(p1_ok, late.per(2, 2, n + 1))
                            nc.gpsimd.tensor_tensor(PART[w][:, 2, :], REST[w][:], PART[w][:, 1, :],
                                                    ALU.subtract).then_inc(p2_ok, 1)
                    if h and done:
                        pool.wait_ge(ve2_ok, done.n(1, 1))
                        nc.gpsimd.tensor_tensor(rs2[:], ve2[:], minus_half, ALU.pow).then_inc(rs2_ok, 1)
                    if t:
                        pool.wait_ge(max_ok, t.n(2, h + 1))
                        s = sc[:, t.slot(4), 1024 * h:1024 * h + 1024].rearrange("p (h k) -> p h k", h=8)
                        m = negmax[:, t.slot(2), 8 * h:8 * h + 8].unsqueeze(2).broadcast_to([P, 8, P])
                        nc.gpsimd.tensor_tensor(s, s, m, ALU.add).then_inc(sub_ok, 1)
                if proj and proj.slot(2) == 1:
                    for n, w in enumerate("qk"):
                        pool.wait_ge(p0_ok, proj.per(2, 2, n + 1))
                        if proj.reached(2):
                            pool.wait_ge(p2_ok, proj.per(2, 2))
                        nc.gpsimd.tensor_tensor(REST[w][:], F[w][:], PART[w][:, 0, :],
                                                ALU.subtract).then_inc(rest_ok, 1)
                t = seq(i, k, 6)
                if t and t.slot(4) == 3:
                    pool.wait_ge(slot_ok, t.per(4, 1, 1))
                    pool.nop(nofuse=True)
                    for j in range(4):
                        nc.gpsimd.indirect_dma_start(
                            list_dram, bass.IndirectOffsetOnAxis(ap=slot_i[:, j:j + 1], axis=0),
                            ids4_i[:, j:j + 1], None).then_inc(ids_out, 16)

            run_steps(pool, FIRST, LAST, U, LOOP, step)
            for q in x2_out:
                pool.wait_ge(q, 16 * (N // 2))

            def fstep(i, k):
                t = tile(i, k, -1)
                if t:
                    pool.wait_ge(veg_ok, t.n(HALVES, HALVES))
                    nc.gpsimd.tensor_tensor(rsg[:], veg[:], minus_half.broadcast_to([P, HALVES]),
                                            ALU.pow).then_inc(rsg_ok, HALVES)
                t = tile(i, k, 2)
                if t:
                    pool.wait_ge(og_ok, t.n(1, 1))
                    pool.nop(nofuse=True)
                    for a in range(HALVES):
                        nc.gpsimd.indirect_dma_start(
                            out_rows, bass.IndirectOffsetOnAxis(ap=ids[:, t.slot(8), a:a + 1], axis=0),
                            og[:, t.slot(2), a, :], None, bounds_check=TOKENS - 1, oob_is_err=False
                        ).then_inc(og_out[t.slot(2)], 16)
                t = tile(i, k, -2)
                if t:
                    pool.wait_ge(idc_ok, t.n(1, 1))
                    if t.reached(4):
                        pool.wait_ge(og_ok, t.n(1, -3))
                    pool.nop(nofuse=True)
                    for a in range(HALVES):
                        nc.gpsimd.indirect_dma_start(
                            xg[:, t.slot(4), a, :], None, x2_dram,
                            bass.IndirectOffsetOnAxis(ap=idc[:, t.slot(4), a:a + 1], axis=0)
                        ).then_inc(xg_in[t.slot(4)], 16)

            run_steps(pool, FFIRST, FLAST, FU, FLOOP, fstep)

        @block.tensor
        def _(pe):
            mm = nc.tensor.matmul
            pe.wait_ge(s_set, 16 * SETUP_DMAS)
            for n, w in enumerate("qkv"):
                for c in range(KC):
                    ins = mm(bank[n][:, c * HID:(c + 1) * HID], A[w][:, c * P:(c + 1) * P], B[w][:],
                             start=True, stop=True)
            ins.then_inc(s_setp, 1)
            pe.wait_ge(s_setd, 9)

            def scores(t, q):
                pair, tok = t.k // 2 % 2, P * t.slot(2)
                if q == 0 and t.slot(2) == 0:
                    pe.wait_ge(qk_in[pair], t.per(4, 32 * len(PAIRS), 32 * len(PAIRS)))
                if q >= 2 or t.reached(1):
                    pe.wait_ge(s_used, t.n(4, q - 1))
                for h in range(4 * q, 4 * q + 4):
                    col = h % 8 * KC + h // 8
                    ins = mm(b_s[q % 2][:, P * (h % 4):P * (h % 4) + P], ST["q"][:, pair, col, tok:tok + P],
                             ST["k"][:, pair, col, tok:tok + P], start=True, stop=True)
                ins.then_inc(s_ready, 1)

            def turn(t, q):
                if q % 2 == 0:
                    pe.wait_ge(sub_ok, t.n(2, q // 2 + 1))
                if q >= 2 or t.reached(1):
                    pe.wait_ge(pt_ready, t.n(4, q - 1))
                for h in range(4):
                    o = 512 * q + P * h
                    ins = nc.tensor.transpose(b_t[q % 2][:, P * h:P * h + P], sc[:, t.slot(4), o:o + P], ident)
                ins.then_inc(tr_ready, 1)

            def step(i, k):
                nxt, cur, prev, old = seq(i, k, -4), seq(i, k, 0), seq(i, k, 1), seq(i, k, 3)
                if nxt:
                    pe.wait_ge(xn_ok, nxt.n(1, 1))
                    pe.wait_ge(ctx_inn[nxt.slot(4)], nxt.per(4, 16, 16))
                    if nxt.reached(1):
                        pe.wait_ge(xt_evac, nxt.n())
                    for c in range(KC):
                        nc.tensor.transpose(b_x[:, c * P:c * P + P],
                                            xn[:, nxt.slot(2), c * P:c * P + P], ident)
                    for c in range(KC):
                        ins = nc.tensor.transpose(b_x[:, (KC + c) * P:(KC + c) * P + P],
                                                  ctx_sb[:, nxt.slot(4), c * P:c * P + P], ident)
                    ins.then_inc(xt_ready, 1)
                for q in range(2):
                    if cur:
                        scores(cur, q)
                    if prev:
                        turn(prev, q)
                if nxt:
                    pair, tok = nxt.k // 2 % 2, P * nxt.slot(2)
                    pe.wait_ge(xt_evac, nxt.n(1, 1))
                    if nxt.reached(1):
                        pe.wait_ge(v_evac, nxt.n())
                    if nxt.slot(2) == 0 and nxt.reached(2):
                        pe.wait_ge(k_evac, nxt.per(2))
                    for c in range(KC):
                        ins = mm(b_vk[:, 0:HID], XT[:, pair, KC + c, tok:tok + P], W["v"][:, c, :],
                                 start=(c == 0), stop=(c == KC - 1))
                    ins.then_inc(v_ready, 1)
                    if nxt.slot(2) == 1:
                        if nxt.reached(8):
                            pe.wait_ge(x2t_evac, nxt.n(1, -7))
                        for o in range(KC):
                            for c in range(KC):
                                ins = mm(b_q[:, 256 * o:256 * o + 256], W["q"][:, c, o * P:o * P + P],
                                         XT[:, pair, c, :], start=(c == 0), stop=(c == KC - 1))
                        ins.then_inc(q_ready, 1)
                        pe.wait_ge(v_evac, nxt.n(1, 1))
                        for o in range(KC):
                            for c in range(KC):
                                ins = mm(b_vk[:, 256 * o:256 * o + 256], W["k"][:, c, o * P:o * P + P],
                                         XT[:, pair, KC + c, :], start=(c == 0), stop=(c == KC - 1))
                        ins.then_inc(k_ready, 1)
                for q in range(2, 4):
                    if cur:
                        scores(cur, q)
                    if prev:
                        turn(prev, q)
                    if q == 2 and old:
                        pe.wait_ge(xn2_ok, old.n(1, 1))
                        if old.reached(1):
                            pe.wait_ge(x2t_evac, old.n())
                        if nxt and nxt.slot(2) == 1:
                            pe.wait_ge(q_evac, nxt.per(2, 1, 1))
                        for c in range(KC):
                            ins = nc.tensor.transpose(b_q[:, c * P:c * P + P],
                                                      xn2[:, old.slot(2), c * P:c * P + P], ident)
                        ins.then_inc(x2t_ready, 1)
                here = At(i, k, U)
                if not here.reached(1) or (isinstance(i, int) and k > N + 4):
                    return
                ins = None
                if here.reached(2):
                    pe.wait_ge(o_used, here.n(1, -1))
                if old:
                    pe.wait_ge(x2t_evac, old.n(1, 1))
                    for c in range(KC):
                        ins = mm(log_ps, x2T[:, old.slot(2), c, :], wg_sb[:, c, :], start=(c == 0), stop=(c == KC - 1))
                grp = seq(i, k, 5)
                if grp and grp.slot(4) == 3:
                    pe.wait_ge(cnt_ok, grp.per(4, 4, 4))
                    mm(pos_ps, tri, OH[:], start=True, stop=False)
                    ins = mm(pos_ps, ones, CNT[:, 0:4, :], start=False, stop=True)
                if prev:
                    pe.wait_ge(pt_ready, prev.n(4, 4))
                    for h in range(HEADS):
                        ins = mm(o_ps[:, h, :], PT[:, P * h:P * h + P], V[:, prev.slot(8), h, :],
                                 start=True, stop=True)
                if ins:
                    ins.then_inc(o_ready, 1)
                else:
                    pe.sem_inc(o_ready, 1)

            run_steps(pe, FIRST, LAST, U, LOOP, step)

            pe.wait_ge(o_used, N + 4)
            mm(b_o[:, 0:EXPERTS], ones, CNT[:, 4, :], start=True, stop=True).then_inc(c_ready, 1)

            def fstep(i, k):
                t = tile(i, k, -1)
                if t:
                    pe.wait_ge(xgn_ok, t.n(HALVES, HALVES))
                    if t.reached(2):
                        pe.wait_ge(gt_evac, t.n(1, -1))
                    for c in range(KC):
                        for a in range(HALVES):
                            o = c * FT + a * P
                            ins = nc.tensor.transpose(bank[t.slot(2)][:, o:o + P],
                                                      xgn[:, t.slot(2), a, c * P:c * P + P], ident)
                    ins.then_inc(gt_ready, 1)
                t = tile(i, k, 0)
                if t:
                    pe.wait_ge(gt_evac, t.n(1, 1))
                    pe.wait_ge(w1_in[t.slot(2)], t.per(2, 32, 32))
                    if t.reached(2):
                        pe.wait_ge(h_ok, t.n(1, -1))
                    for o in range(KC):
                        for c in range(KC):
                            ins = mm(bank[2 + t.slot(2)][:, FT * o:FT * o + FT], w1_sb[:, t.slot(2), c, o * P:o * P + P],
                                     xgT[:, t.slot(2), c, :], start=(c == 0), stop=(c == KC - 1))
                    ins.then_inc(h_ready, 1)
                t = tile(i, k, 1)
                if t:
                    pe.wait_ge(h_ok, t.n(1, 1))
                    pe.wait_ge(w2_in[t.slot(4)], t.per(4, 32, 32))
                    if t.reached(2):
                        pe.wait_ge(y_used, t.n(1, -1))
                    for a in range(HALVES):
                        for c in range(KC):
                            ins = mm(bank[6 + t.slot(2)][:, HID * a:HID * a + HID],
                                     hT[:, t.slot(2), c, a * P:a * P + P], w2_sb[:, t.slot(4), c, :],
                                     start=(c == 0), stop=(c == KC - 1))
                    ins.then_inc(y_ready, 1)

            run_steps(pe, FFIRST, FLAST, FU, FLOOP, fstep)

        @block.scalar
        def _(act):
            act.wait_ge(s_set, 16 * SETUP_DMAS)
            nc.scalar.activation(tg[:], g_raw[:], ACT.Tanh).then_inc(s_seta, 1)
            act.wait_ge(s_setd, 9)
            act.wait_ge(s_setg, 2)

            def step(i, k):
                nxt, prev, old, late = seq(i, k, -4), seq(i, k, 1), seq(i, k, 3), seq(i, k, -2)
                if nxt:
                    pair, tok = nxt.k // 2 % 2, P * nxt.slot(2)
                    act.wait_ge(xt_ready, nxt.n(1, 1))
                    if nxt.reached(4):
                        act.wait_ge(k_ready, nxt.per(2, 1, -1))
                    nc.scalar.copy(XT[:, pair, :, tok:tok + P],
                                   b_x[:].rearrange("p (c t) -> p c t", t=P)).then_inc(xt_evac, 1)

                if late and late.slot(2) == 0:
                    for n, w in enumerate("qk"):
                        act.wait_ge(rest_ok, late.per(2, 2, n + 1))
                        nc.scalar.copy(PART[w][:, 1, :], REST[w][:]).then_inc(p1_ok, 1)

                def probs(q):
                    act.wait_ge(tr_ready, prev.n(4, q + 1))
                    if q == 0 and prev.reached(1):
                        act.wait_ge(o_ready, prev.n())
                    nc.scalar.activation(PT[:, 512 * q:512 * q + 512], b_t[q % 2][:], ACT.Exp).then_inc(pt_ready, 1)

                if prev:
                    probs(0)
                    probs(1)
                if nxt:
                    act.wait_ge(v_ready, nxt.n(1, 1))
                    if nxt.reached(8):
                        act.wait_ge(o_ready, nxt.n(1, -7))
                    nc.scalar.copy(V[:, nxt.slot(8), :, 0:D],
                                   b_vk[:, 0:HID].rearrange("p (h d) -> p h d", d=D)).then_inc(v_evac, 1)
                    if nxt.slot(2) == 1:
                        for n, (w, ps, ready, evac, col) in enumerate((("q", b_q, q_ready, q_evac, bq_col),
                                                                       ("k", b_vk, k_ready, k_evac, bk_col))):
                            act.wait_ge(ready, nxt.per(2, 1, 1))
                            if nxt.reached(2):
                                act.wait_ge(rest_ok, nxt.per(2, 2))
                                act.wait_ge(qk_in[(nxt.k // 2 + 1) % 2],
                                            nxt.minus(2).per(4, 32 * len(PAIRS), 32 * len(PAIRS)))
                            for o in range(KC):
                                ins = nc.scalar.activation(F[w][:, 256 * o:256 * o + 256],
                                                           ps[:, 256 * o:256 * o + 256],
                                                           ACT.Identity, bias=col[:, o:o + 1])
                            ins.then_inc(evac, 1)
                            act.wait_ge(evac, nxt.per(2, 1, 1))
                            nc.scalar.copy(PART[w][:, 0, :], F[w][:]).then_inc(p0_ok, 1)
                if prev:
                    probs(2)
                if old:
                    act.wait_ge(x2t_ready, old.n(1, 1))
                    if old.reached(2):
                        act.wait_ge(o_ready, old.n(1, 1))
                    nc.scalar.copy(x2T[:, old.slot(2)], b_q[:, 0:HID].rearrange("p (c t) -> p c t", t=P)
                                   ).then_inc(x2t_evac, 1)
                if prev:
                    probs(3)

            run_steps(act, FIRST, LAST, U, LOOP, step)

            def fstep(i, k):
                t = tile(i, k, -1)
                if t:
                    act.wait_ge(gt_ready, t.n(1, 1))
                    if t.reached(2):
                        act.wait_ge(h_ready, t.n(1, -1))
                    nc.scalar.copy(xgT[:, t.slot(2)], bank[t.slot(2)][:].rearrange("p (c t) -> p c t", t=FT)
                                   ).then_inc(gt_evac, 1)
                t = tile(i, k, 0)
                if t:
                    act.wait_ge(h_ready, t.n(1, 1))
                    if t.reached(2):
                        act.wait_ge(y_ready, t.n(1, -1))
                    for o in range(KC):
                        ins = nc.scalar.activation(hT[:, t.slot(2), o, :], bank[2 + t.slot(2)][:, FT * o:FT * o + FT],
                                                   ACT.Gelu, bias=b1_sb[:, t.slot(2), o:o + 1])
                    ins.then_inc(h_ok, 1)

            run_steps(act, FFIRST, FLAST, FU, FLOOP, fstep)

        @block.vector
        def _(dve):
            dve.wait_ge(s_set, 16 * SETUP_DMAS)
            dve.wait_ge(s_setp, 1)
            dve.wait_ge(s_seta, 1)
            for n, w in enumerate("qkv"):
                nc.vector.scalar_tensor_tensor(out=W[w][:], in0=bank[n][:].rearrange("p (c h) -> p c h", c=KC),
                                               scalar=LORA, in1=W[w][:], op0=ALU.mult, op1=ALU.add).then_inc(s_setd, 1)
            nc.vector.memset(CNT[:], 0.0).then_inc(s_setd, 1)
            nc.vector.memset(zero8[:], 0.0).then_inc(s_setd, 1)
            dve.wait_ge(s_setd, 5)
            nc.vector.tensor_scalar(W["q"][:], W["q"][:], D ** -0.5, None, ALU.mult).then_inc(s_setd, 1)
            nc.vector.tensor_scalar(bq_col[:], bq_col[:], D ** -0.5, None, ALU.mult).then_inc(s_setd, 1)
            nc.vector.tensor_scalar(W["v"][:], W["v"][:], tg[:, 0:1], None, ALU.mult).then_inc(s_setd, 1)
            nc.vector.tensor_scalar(bv_all[:], bv_all[:], tg[:, 0:1], None, ALU.mult).then_inc(s_setd, 1)
            dve.wait_ge(s_setd, 9)

            def row_stats(src, st, mv, ve, st_s, mv_s, ve_s, at):
                nc.vector.bn_stats(st, src).then_inc(st_s, 1)
                dve.wait_ge(st_s, at)
                dve.nop(nofuse=True)
                nc.vector.bn_aggr(mv, st).then_inc(mv_s, 1)
                dve.wait_ge(mv_s, at)
                nc.vector.tensor_scalar(ve, mv[:, 1:2], EPS, None, ALU.add).then_inc(ve_s, 1)

            def row_apply(src, dst, mv, rs, rs_s, done, at, free=None):
                dve.wait_ge(rs_s, at)
                if free:
                    dve.wait_ge(*free)
                nc.vector.tensor_scalar(dst, src, mv[:, 0:1], rs, ALU.subtract, ALU.mult).then_inc(done, 1)

            def add_bias(t, q):
                if q == 0:
                    dve.wait_ge(bias_in[t.slot(4)], t.per(4, 32, 32))
                dve.wait_ge(s_ready, t.n(4, q + 1))
                s = sc[:, t.slot(4), 512 * q:512 * q + 512]
                nc.vector.tensor_tensor(s, b_s[q % 2][:], s, ALU.add).then_inc(s_used, 1)

            def row_max(t, h):
                dve.wait_ge(s_used, t.n(4, 2 * h + 2))
                if h == 0 and t.reached(2):
                    dve.wait_ge(sub_ok, t.n(2, -2))
                nc.vector.tensor_reduce(
                    negmax[:, t.slot(2), 8 * h:8 * h + 8],
                    sc[:, t.slot(4), 1024 * h:1024 * h + 1024].rearrange("p (h k) -> p h k", h=8),
                    AX.X, ALU.max, negate=True).then_inc(max_ok, 1)

            def step(i, k):
                cur, done, gate, ahead = seq(i, k, 0), seq(i, k, 2), seq(i, k, 4), seq(i, k, -5)
                here = At(i, k, U)
                if ahead:
                    dve.wait_ge(x_in[ahead.slot(4)], ahead.per(4, 16, 16))
                    row_stats(x_sb[:, ahead.slot(4), :], st1[:], mv1[:], ve1[:], st1_ok, mv1_ok, ve1_ok,
                              ahead.n(1, 1))
                if cur:
                    add_bias(cur, 0)
                    add_bias(cur, 1)
                    row_max(cur, 0)
                if here.reached(2):
                    dve.wait_ge(o_ready, here.n(1, -1))
                    if gate:
                        if gate.slot(4) == 0 and gate.reached(4):
                            dve.wait_ge(oh_ok, gate.per(4))
                        ins = nc.vector.tensor_tensor(L[:, gate.slot(4), :], log_ps, bg_all[:], ALU.add)
                        ins.then_inc(l_ok, 1)
                    grp = seq(i, k, 6)
                    if grp and grp.slot(4) == 3:
                        g = grp.per(4, 1, 1)
                        if grp.reached(7):
                            dve.wait_ge(ids4_next, grp.per(4))
                        ins = nc.vector.tensor_tensor(where[:], pos_ps, ebase, ALU.add)
                        ins.then_inc(pos_ok, 1)
                        dve.wait_ge(pos_ok, g)
                        nc.vector.tensor_tensor(where[:], where[:], OH[:], ALU.mult).then_inc(where_ok, 1)
                        dve.wait_ge(where_ok, g)
                        nc.vector.tensor_reduce(slot_f[:], where[:], AX.X, ALU.add).then_inc(slotf_ok, 1)
                        dve.wait_ge(slotf_ok, g)
                        if grp.reached(7):
                            dve.wait_ge(ids_out, grp.per(4, 64))
                        nc.vector.tensor_copy(ids4_i[:], ids4[:]).then_inc(ids4_ok, 1)
                        nc.vector.tensor_copy(slot_i[:], slot_f[:]).then_inc(slot_ok, 1)
                        dve.wait_ge(ids4_ok, g)
                        nc.vector.tensor_scalar(ids4[:], ids4[:], float(4 * P), None, ALU.add).then_inc(ids4_next, 1)
                    if done:
                        nc.vector.reciprocal(rden[:], o_ps[:, :, D]).then_inc(rden_ok, 1)
                        dve.wait_ge(rden_ok, done.n(1, 1))
                        if done.reached(2):
                            dve.wait_ge(x2_out[done.slot(2)], done.per(2, 16))
                        y = x2[:, done.slot(2), :]
                        nc.vector.tensor_tensor(y.rearrange("p (h d) -> p h d", d=D), o_ps[:, :, 0:D],
                                                rden[:].unsqueeze(2).broadcast_to([P, HEADS, D]),
                                                ALU.mult).then_inc(o_used, 1)
                        dve.wait_ge(o_used, here.n(1, -1))
                        dve.wait_ge(xr_ok, done.n(1, 1))
                        nc.vector.tensor_tensor(y, y, xr[:, done.slot(8), :], ALU.add).then_inc(x2_ok, 1)
                        dve.wait_ge(x2_ok, done.n(1, 1))
                        row_stats(y, st2[:], mv2[:], ve2[:], st2_ok, mv2_ok, ve2_ok, done.n(1, 1))
                    else:
                        if gate:
                            dve.wait_ge(l_ok, gate.n(1, 1))
                        dve.sem_inc(o_used, 1)
                if cur:
                    add_bias(cur, 2)
                    add_bias(cur, 3)
                    row_max(cur, 1)
                if ahead:
                    row_apply(x_sb[:, ahead.slot(4), :], xn[:, ahead.slot(2), :], mv1[:], rs1[:], rs1_ok, xn_ok,
                              ahead.n(1, 1), (xt_ready, ahead.n(1, -1)) if ahead.reached(2) else None)
                if done:
                    row_apply(x2[:, done.slot(2), :], xn2[:, done.slot(2), :], mv2[:], rs2[:], rs2_ok, xn2_ok,
                              done.n(1, 1), (x2t_ready, done.n(1, -1)) if done.reached(2) else None)
                if gate and gate.slot(4) == 3:
                    g = gate.per(4, 1, 1)
                    dve.wait_ge(l_ok, gate.n(1, 1))
                    nc.vector.tensor_reduce(lmax[:], L[:], AX.X, ALU.max).then_inc(lmax_ok, 1)
                    dve.wait_ge(lmax_ok, g)
                    nc.vector.tensor_tensor(key[:], L[:], lmax[:].unsqueeze(2).broadcast_to([P, 4, EXPERTS]),
                                            ALU.is_lt).then_inc(lt_ok, 1)
                    dve.wait_ge(lt_ok, g)
                    nc.vector.scalar_tensor_tensor(out=key[:], in0=key[:], scalar=float(2 * EXPERTS), in1=iota,
                                                   op0=ALU.mult, op1=ALU.add).then_inc(key_ok, 1)
                    dve.wait_ge(key_ok, g)
                    nc.vector.tensor_reduce(pick[:], key[:], AX.X, ALU.min).then_inc(pick_ok, 1)
                    dve.wait_ge(pick_ok, g)
                    nc.vector.tensor_tensor(OH[:], iota, pick[:].unsqueeze(2).broadcast_to([P, 4, EXPERTS]),
                                            ALU.is_equal).then_inc(oh_ok, 1)
                    nc.vector.tensor_copy(CNT[:, 0, :], CNT[:, 4, :]).then_inc(cnt0_ok, 1)
                    dve.wait_ge(oh_ok, g)
                    dve.wait_ge(cnt0_ok, g)
                    for j in range(4):
                        nc.vector.tensor_tensor(CNT[:, j + 1, :], CNT[:, j, :], OH[:, j, :], ALU.add).then_inc(cnt_ok, 1)
                        dve.wait_ge(cnt_ok, gate.per(4, 4, j + 1))

            run_steps(dve, FIRST, LAST, U, LOOP, step)

            made = [0]

            def link(ins):
                made[0] += 1
                ins.then_inc(s_tab, 1)
                dve.wait_ge(s_tab, made[0])

            M = TOKENS // FT
            dve.wait_ge(c_ready, 1)
            link(nc.vector.tensor_copy(cnt[:], b_o[0:1, 0:EXPERTS]))
            link(nc.vector.tensor_tensor(over[:], cnt[:].unsqueeze(2).broadcast_to([1, EXPERTS, M]),
                                         row[:, R_M:R_J].rearrange("p (e m) -> p e m", m=M), ALU.is_gt))
            link(nc.vector.tensor_reduce(nt[:], over[:], AX.X, ALU.add))
            link(nc.vector.tensor_tensor_scan(end[:], nt[:], zero8[:], 0.0, ALU.add, ALU.add))
            link(nc.vector.tensor_tensor(past[:], row[:, R_J:R_J256].rearrange("p (j e) -> p j e", e=EXPERTS),
                                         end[:].unsqueeze(1).broadcast_to([1, TILES, EXPERTS]), ALU.is_ge))
            link(nc.vector.tensor_tensor(ptn[:], past[:], nt[:].unsqueeze(1).broadcast_to([1, TILES, EXPERTS]),
                                         ALU.mult))
            link(nc.vector.tensor_reduce(e_f[:], past[:], AX.X, ALU.add))
            link(nc.vector.tensor_reduce(s_f[:], ptn[:], AX.X, ALU.add))
            link(nc.vector.scalar_tensor_tensor(out=b_f[:], in0=s_f[:], scalar=float(-FT), in1=row[:, R_J256:R_END],
                                                op0=ALU.mult, op1=ALU.add))
            link(nc.vector.scalar_tensor_tensor(out=b_f[:], in0=e_f[:], scalar=float(TOKENS), in1=b_f[:],
                                                op0=ALU.mult, op1=ALU.add))
            link(nc.vector.tensor_scalar(ec_f[:], e_f[:], float(EXPERTS - 1), None, ALU.min))
            link(nc.vector.tensor_copy(tile_e[:], ec_f[:]))
            nc.vector.tensor_copy(tile_b[:], b_f[:]).then_inc(tab_ok, 1)

            def fstep(i, k):
                t = tile(i, k, -2)
                if t:
                    dve.wait_ge(ids_in[t.slot(8)], t.per(8, 16, 16))
                    if t.reached(4):
                        dve.wait_ge(xg_in[t.slot(4)], t.per(4, 32))
                    nc.vector.tensor_scalar(idc[:, t.slot(4), :], ids[:, t.slot(8), :], float(TOKENS - 1), None,
                                            ALU.min).then_inc(idc_ok, 1)
                t = tile(i, k, -1)
                if t:
                    dve.wait_ge(xg_in[t.slot(4)], t.per(4, 32, 32))
                    for a in range(HALVES):
                        row_stats(xg[:, t.slot(4), a, :], stg[:, a, :], mvg[:, a, :], veg[:, a:a + 1],
                                  stg_ok, mvg_ok, veg_ok, t.n(HALVES, a + 1))
                t = tile(i, k, 2)
                if t:
                    dve.wait_ge(y_ready, t.n(1, 1))
                    if t.reached(1):
                        dve.wait_ge(og_ok, t.n())
                    nc.vector.tensor_tensor(yb[:], bank[6 + t.slot(2)][:].rearrange("p (a h) -> p a h", a=HALVES),
                                            b2_sb[:, t.slot(4), :].unsqueeze(1).broadcast_to([P, HALVES, HID]),
                                            ALU.add).then_inc(y_used, 1)
                    dve.wait_ge(y_used, t.n(1, 1))
                    if t.reached(2):
                        dve.wait_ge(og_out[t.slot(2)], t.per(2, 16 * HALVES))
                    nc.vector.scalar_tensor_tensor(out=og[:, t.slot(2)].rearrange("p a h -> p (a h)"),
                                                   in0=yb[:].rearrange("p a h -> p (a h)"), scalar=tg[:, 1:2],
                                                   in1=xg[:, t.slot(4)].rearrange("p a h -> p (a h)"),
                                                   op0=ALU.mult, op1=ALU.add).then_inc(og_ok, 1)
                t = tile(i, k, -1)
                if t:
                    for a in range(HALVES):
                        row_apply(xg[:, t.slot(4), a, :], xgn[:, t.slot(2), a, :], mvg[:, a, :], rsg[:, a:a + 1],
                                  rsg_ok, xgn_ok, t.n(HALVES, a + 1),
                                  (gt_ready, t.n(1, -1)) if a == 0 and t.reached(2) else None)

            run_steps(dve, FFIRST, FLAST, FU, FLOOP, fstep)


def kernel(**inputs):
    import numpy as np
    import concourse.bacc as bacc
    from concourse.bass_utils import run_bass_kernel_spmd

    a = {k: np.ascontiguousarray(v) for k, v in inputs.items()}

    def chunks(m):
        return np.ascontiguousarray(m.reshape(KC, P, -1).transpose(1, 0, 2))

    arrays = {
        "x": a["x"], "ctx_in": a["ctx_1024"], "bias": a["fside_Bx16xSxS2_0"],
        "g_xattn": a["g_xattn"].reshape(1), "g_ffn": a["g_ffn"].reshape(1),
    }
    def heads_inside(m):
        return np.ascontiguousarray(m.reshape(-1, KC, 8, D).transpose(0, 1, 3, 2).reshape(-1, HID))

    for w in "qkv":
        wt, b, bt = a[f"L0_xattn_W{w}"].T, a[f"L0_xattn_b{w}"], a[f"L0_xattn_B{w}"].T
        if w != "v":
            wt, b, bt = heads_inside(wt), np.ascontiguousarray(heads_inside(b).reshape(KC, P).T), heads_inside(bt)
        arrays[f"w{w}T"], arrays[f"b{w}"], arrays[f"b{w}T"] = chunks(wt), b, np.ascontiguousarray(bt)
        arrays[f"a{w}"] = a[f"L0_xattn_A{w}"]
    arrays["wg"] = chunks(a["L0_ffn_Wg"])
    arrays["bg"] = a["L0_ffn_bg"].reshape(1, EXPERTS)
    arrays["w1"] = np.stack([chunks(m) for m in a["L0_ffn_W1"]])
    arrays["b1"] = np.ascontiguousarray(a["L0_ffn_b1"].reshape(EXPERTS, KC, P).transpose(0, 2, 1))
    arrays["w2"] = np.stack([chunks(m) for m in a["L0_ffn_W2"]])
    arrays["b2"] = a["L0_ffn_b2"]

    c = np.zeros((P, C_END), np.float32)
    c[:, C_ID:C_ID + P] = np.eye(P)
    c[:, C_TRI:C_TRI + P] = np.triu(np.ones((P, P)), 1)
    c[:, C_ONE:C_ONE + P] = 1
    c[:, C_HALF] = -0.5
    c[:, C_IOTA:C_IOTA + 32] = np.tile(np.arange(EXPERTS), 4)
    c[:, C_BASE:C_BASE + 32] = np.tile(np.arange(EXPERTS) * TOKENS, 4)
    r = np.zeros((1, R_END), np.float32)
    r[0, R_M:R_J] = np.tile(np.arange(TOKENS // FT) * FT, EXPERTS)
    r[0, R_J:R_J256] = np.repeat(np.arange(TILES), EXPERTS)
    r[0, R_J256:R_END] = np.arange(TILES) * FT
    arrays["consts"], arrays["row_consts"] = c, r
    arrays["ids_const"] = (np.arange(P)[:, None] + P * np.arange(4)[None, :]).astype(np.float32)

    nc = bacc.Bacc("TRN2", target_bir_lowering=False, num_devices=1)
    order = ["x", "ctx_in", "bias", "g_xattn", "g_ffn", "wqT", "bq", "aq", "bqT", "wkT", "bk", "ak", "bkT",
             "wvT", "bv", "av", "bvT", "wg", "bg", "w1", "b1", "w2", "b2", "consts", "row_consts", "ids_const"]
    aps = [nc.dram_tensor(f"in_{n}", arrays[n].shape, mybir.dt.from_np(arrays[n].dtype), kind="ExternalInput").ap()
           for n in order]
    out = nc.dram_tensor("out_0", (N, P, HID), F32, kind="ExternalOutput").ap()
    flamingo_block(nc, *aps, out)
    r = run_bass_kernel_spmd(nc, [{f"in_{n}": arrays[n] for n in order}], core_ids=[0])
    return r.results[0]["out_0"]
```

```python
from contextlib import ExitStack

import concourse.bass as bass
from concourse import mybir

F32 = mybir.dt.float32
I32 = mybir.dt.int32
BF16 = mybir.dt.bfloat16
ALU = mybir.AluOpType
ACT = mybir.ActivationFunctionType
AX = mybir.AxisListType

P = 128
N = 128
HID = 256
KC = HID // P
HEADS = 16
D = HID // HEADS
RANK = 8
LORA = 16.0 / RANK
EXPERTS = 8
EPS = 1e-5
TOKENS = N * P
U = 8

FT = 256
HALVES = FT // P
TILES = 72
FU = 8
NO_TOKEN = 1 << 20
LIST = EXPERTS * TOKENS + TILES * FT

PAIRS = [(0, 0), (0, 1), (0, 2), (1, 0), (1, 1), (2, 0)]
ROWS = D * len(PAIRS)
CELL = 32

C_ID, C_TRI, C_ONE, C_IOTA, C_BASE = 0, 128, 256, 384, 416
C_HALF = 448
C_END = 449
R_M, R_J, R_J256 = 0, EXPERTS * (TOKENS // FT), EXPERTS * (TOKENS // FT) + TILES * EXPERTS
R_END = R_J256 + TILES


class At:

    def __init__(self, i, k, width):
        self.i, self.k, self.width = i, k, width

    def slot(self, m):
        return self.k % m

    def n(self, mul=1, add=0):
        v = self.k * mul + add
        return self.i * (self.width * mul) + v

    def per(self, m, mul=1, add=0):
        v = (self.k // m) * mul + add
        return self.i * (self.width // m * mul) + v

    def minus(self, lag):
        return At(self.i, self.k - lag, self.width)

    def reached(self, least):
        return not isinstance(self.i, int) or self.i * self.width + self.k >= least


def run_steps(eng, first, last, width, loop_rounds, body):
    a, b = loop_rounds
    for s in range(first, a * width):
        body(0, s)
    with eng.Fori(a, b) as i:
        for k in range(width):
            body(i, k)
    for s in range(b * width, last + 1):
        body(0, s)


def flamingo_block(nc, x, ctx_in, bias, g_xattn, g_ffn, wqT, bq, aq, bqT, wkT, bk, ak, bkT, wvT, bv, av, bvT,
                   wg, bg, w1, w2, b2, consts, row_consts, ids_const, out):
    ctx = ExitStack()
    with ctx:
        def sb(name, shape, dt=F32):
            return ctx.enter_context(nc.sbuf_tensor(name, shape, dt))

        def sem(name):
            return ctx.enter_context(nc.semaphore(name))

        x2_dram = nc.dram_tensor("x2_dram", (TOKENS, HID), F32, kind="Internal").ap()
        list_dram = nc.dram_tensor("list_dram", (LIST, 1), I32, kind="Internal").ap()

        cst = sb("cst", [P, C_END])
        row = sb("row", [1, R_END])
        ids4 = sb("ids4", [P, 4])
        ids4_i = sb("ids4_i", [P, 4], I32)
        empty = sb("empty", [P, LIST // P], I32)
        ident, tri, ones = cst[:, C_ID:C_ID + P], cst[:, C_TRI:C_TRI + P], cst[:, C_ONE:C_ONE + P]
        minus_half = cst[:, C_HALF:C_HALF + 1]
        iota = cst[:, C_IOTA:C_IOTA + 32].rearrange("p (j e) -> p j e", e=EXPERTS)
        ebase = cst[:, C_BASE:C_BASE + 32].rearrange("p (j e) -> p j e", e=EXPERTS)
        W = {w: sb(f"w{w}", [P, KC, HID]) for w in "qkv"}
        A = {w: sb(f"a{w}", [RANK, HID]) for w in "qkv"}
        B = {w: sb(f"b{w}", [RANK, HID]) for w in "qkv"}
        bq_col = sb("bq_col", [P, KC])
        bk_col = sb("bk_col", [P, KC])
        bv_row = sb("bv_row", [1, HID])
        bg_all = sb("bg_all", [P, EXPERTS])
        wg_sb = sb("wg_sb", [P, KC, EXPERTS])
        g_raw = sb("g_raw", [P, 2])
        tg = sb("tg", [P, 2])

        x_sb = sb("x_sb", [P, 8, HID])
        ctx_sb = sb("ctx_sb", [P, 4, HID])
        sc = sb("sc", [P, 4, HEADS * P])
        xn = sb("xn", [P, 2, HID])
        XT = sb("XT", [P, 2, 2 * KC, 2 * P])
        F = {w: sb(f"f{w}", [P, KC * 2 * P]) for w in "qk"}
        REST = {w: sb(f"rest{w}", [P, KC * 2 * P]) for w in "qk"}
        PART = {w: sb(f"part{w}", [P, 3, KC * 2 * P], BF16) for w in "qk"}
        ST = {w: sb(f"st{w}", [ROWS, 2, HEADS, 2 * P], BF16) for w in "qk"}
        V = sb("V", [P, 8, HEADS, CELL])
        PT = sb("PT", [P, 2, HEADS * P])
        OT = sb("OT", [P, HEADS // 4 * P])
        negmax = sb("negmax", [P, 2, HEADS])
        rden = sb("rden", [P, HEADS])
        x2 = sb("x2", [P, 2, HID])
        xn2 = sb("xn2", [P, 2, HID])
        x2T = sb("x2T", [P, 2, KC, P])
        st, mv = sb("st", [P, 2, 6]), sb("mv", [P, 2, 2])
        ve, rs = sb("ve", [P, 2, 1]), sb("rs", [P, 2, 1])
        L = sb("L", [P, 4, EXPERTS])
        lmax, key, pick = sb("lmax", [P, 4]), sb("key", [P, 4, EXPERTS]), sb("pick", [P, 4])
        OH = sb("OH", [P, 4, EXPERTS])
        CNT = sb("CNT", [P, 5, EXPERTS])
        where = sb("where", [P, 4, EXPERTS])
        slot_f = sb("slot_f", [P, 4])
        slot_i = sb("slot_i", [P, 4], I32)

        cnt = sb("cnt", [1, EXPERTS])
        over = sb("over", [1, EXPERTS, TOKENS // FT])
        nt = sb("nt", [1, EXPERTS])
        zero8 = sb("zero8", [1, EXPERTS])
        end = sb("end", [1, EXPERTS])
        past = sb("past", [1, TILES, EXPERTS])
        ptn = sb("ptn", [1, TILES, EXPERTS])
        e_f, s_f, b_f, ec_f = (sb(t, [1, TILES]) for t in ("e_f", "s_f", "b_f", "ec_f"))
        tile_e = sb("tile_e", [1, TILES], I32)
        tile_b = sb("tile_b", [1, TILES], I32)
        ids = sb("ids", [P, 8, HALVES], I32)
        idc = sb("idc", [P, 4, HALVES], I32)
        old_sc = sc[:].rearrange("p s c -> p (s c)")
        xg = old_sc[:, 0:8 * FT * KC].rearrange("p (s a h) -> p s a h", s=8, a=HALVES)
        w2_sb = old_sc[:, 8 * FT * KC:12 * FT * KC].rearrange("p (s w) -> p s w", s=4)
        xgn = sb("xgn", [P, 2, HALVES, HID])
        xgT = sb("xgT", [P, 2, KC, FT])
        hT = sb("hT", [P, 2, KC, FT])
        w1_sb = sb("w1_sb", [P, 4, KC * HID + KC])
        b2_sb = sb("b2_sb", [1, 4, HID])
        stg, mvg = sb("stg", [P, HALVES, 6]), sb("mvg", [P, HALVES, 2])
        veg, rsg = sb("veg", [P, HALVES]), sb("rsg", [P, HALVES])
        og = sb("og", [P, 2, HALVES, HID])

        bank = [ctx.enter_context(nc.psum_tensor(f"bank{i}", [P, 512], F32)) for i in range(8)]
        b_s, b_t = bank[0:2], bank[2:4]
        b_o, b_x, b_vk, b_q = bank[4], bank[5], bank[6], bank[7]
        o_ps = b_o[:].rearrange("p (h c) -> p h c", c=CELL)
        log_ps = o_ps[:, 0, D + 4:D + 4 + EXPERTS]
        pos_ps = o_ps[:, 1:HEADS:4, D + 4:D + 4 + EXPERTS]

        s_set = sem("s_set")
        s_list0 = sem("s_list0")
        s_setp, s_setd, s_seta, s_setg = sem("s_setp"), sem("s_setd"), sem("s_seta"), sem("s_setg")
        x_in = [sem(f"x_in{i}") for i in range(8)]
        ctx_inn = [sem(f"ctx_in{i}") for i in range(4)]
        bias_in = [sem(f"bias_in{i}") for i in range(4)]
        st_ok, mv_ok = [sem(f"st_ok{i}") for i in range(2)], [sem(f"mv_ok{i}") for i in range(2)]
        ve_ok, rs_ok, xn_ok, xn2_ok = (sem(t) for t in ("ve_ok", "rs_ok", "xn_ok", "xn2_ok"))
        xt_ready, xt_evac = sem("xt_ready"), sem("xt_evac")
        v_ready, v_evac = sem("v_ready"), sem("v_evac")
        q_ready, q_evac, k_ready, k_evac = sem("q_ready"), sem("q_evac"), sem("k_ready"), sem("k_evac")
        p0_ok, p1_ok, rest_ok, p2_ok = sem("p0_ok"), sem("p1_ok"), sem("rest_ok"), sem("p2_ok")
        qk_in = [sem(f"qk_in{i}") for i in range(2)]
        s_ready, s_used, max_ok, sub_ok = sem("s_ready"), sem("s_used"), sem("max_ok"), sem("sub_ok")
        tr_ready, pt_ready = sem("tr_ready"), sem("pt_ready")
        o_ready, o_used = sem("o_ready"), sem("o_used")
        ot_ready, ot_evac = sem("ot_ready"), sem("ot_evac")
        rden_ok, x2_ok = sem("rden_ok"), sem("x2_ok")
        x2_out = [sem(f"x2_out{i}") for i in range(2)]
        x2t_ready, x2t_evac = sem("x2t_ready"), sem("x2t_evac")
        l_ok, lmax_ok, lt_ok, key_ok, pick_ok, oh_ok, cnt0_ok, cnt_ok = (
            sem(t) for t in ("l_ok", "lmax_ok", "lt_ok", "key_ok", "pick_ok", "oh_ok", "cnt0_ok", "cnt_ok"))
        ids4_ok, ids4_next = sem("ids4_ok"), sem("ids4_next")
        pos_ok, where_ok, slotf_ok, slot_ok, ids_out = (
            sem(t) for t in ("pos_ok", "where_ok", "slotf_ok", "slot_ok", "ids_out"))
        c_ready, s_tab, tab_ok = sem("c_ready"), sem("s_tab"), sem("tab_ok")
        ids_in = [sem(f"ids_in{i}") for i in range(8)]
        w1_in = [sem(f"w1_in{i}") for i in range(4)]
        w2_in = [sem(f"w2_in{i}") for i in range(4)]
        idc_ok = sem("idc_ok")
        xg_in = [sem(f"xg_in{i}") for i in range(8)]
        stg_ok, mvg_ok, veg_ok, rsg_ok, xgn_ok = (sem(t) for t in ("stg_ok", "mvg_ok", "veg_ok", "rsg_ok", "xgn_ok"))
        gt_ready, gt_evac, h_ready, h_ok, y_ready, og_ok = (
            sem(t) for t in ("gt_ready", "gt_evac", "h_ready", "h_ok", "y_ready", "og_ok"))
        og_out = [sem(f"og_out{i}") for i in range(2)]

        SETUP_DMAS = 20
        x_seq = x.rearrange("(a n) s h -> n s (a h)", a=1)
        ctx_seq = ctx_in.rearrange("(a n) s h -> n s (a h)", a=1)
        bias_seq = bias.rearrange("n h q k -> n q h k")
        x2_seq = x2_dram.rearrange("(n s) h -> n s h", s=P)
        out_rows = out.rearrange("n s h -> (n s) h")

        LOOP = (1, N // U - 1)
        FIRST, LAST = -6, N + 5
        FLOOP = (1, TILES // FU - 1)
        FFIRST, FLAST = -5, TILES + 1

        block = ctx.enter_context(nc.Block())

        def seq(i, k, lag):
            t = At(i, k - lag, U)
            if isinstance(i, int) and not 0 <= i * U + k - lag < N:
                return None
            return t

        def tile(i, k, lag):
            t = At(i, k - lag, FU)
            if isinstance(i, int) and not 0 <= i * FU + k - lag < TILES:
                return None
            return t

        def norms_at(i, k):
            which = [n for n, lag in enumerate((-5, 2)) if seq(i, k, lag)]
            return (which[0], which[-1] + 1) if which else None

        @block.sync
        def _(sp):
            def load(dst, src):
                sp.dma_start(dst, src).then_inc(s_set, 16)

            load(cst[:], consts)
            load(row[:], row_consts)
            load(ids4[:], ids_const)
            for w, wt, a, b in (("q", wqT, aq, bqT), ("k", wkT, ak, bkT), ("v", wvT, av, bvT)):
                load(W[w][:], wt)
                load(A[w][:], a)
                load(B[w][:], b)
            load(bq_col[:], bq)
            load(bk_col[:], bk)
            load(bv_row[:], bv)
            load(bg_all[:], bg.partition_broadcast(P))
            load(wg_sb[:], wg)
            load(g_raw[:, 0:1], g_xattn.partition_broadcast(P))
            load(g_raw[:, 1:2], g_ffn.partition_broadcast(P))
            load(cnt[:], bg)
            sp.wait_ge(s_setg, 1)
            sp.dma_start(list_dram.rearrange("(p c) o -> p (c o)", p=P), empty[:]).then_inc(s_list0, 16)

            def step(i, k):
                t = seq(i, k, -6)
                if t:
                    if t.reached(4):
                        sp.wait_ge(xt_ready, t.n(1, -3))
                        sp.nop(nofuse=True)
                    sp.dma_start(ctx_sb[:, t.slot(4), :], ctx_seq[t.n()]).then_inc(ctx_inn[t.slot(4)], 16)
                    if t.reached(8):
                        sp.wait_ge(x2_ok, t.n(1, -7))
                        sp.nop(nofuse=True)
                        sp.wait_ge(xn_ok, t.n(1, -7))
                        sp.nop(nofuse=True)
                    sp.dma_start(x_sb[:, t.slot(8), :], x_seq[t.n()]).then_inc(x_in[t.slot(8)], 16)
                t = seq(i, k, -2)
                if t and t.slot(2) == 0:
                    pair = t.k // 2 % 2
                    sp.wait_ge(p2_ok, t.per(2, 2, 2))
                    sp.nop(nofuse=True)
                    if t.reached(4):
                        sp.wait_ge(s_ready, t.n(4, -8))
                    sp.nop(nofuse=True)
                    for w, which in (("q", 0), ("k", 1)):
                        for r, parts in enumerate(PAIRS):
                            sp.dma_start(ST[w][D * r:D * r + D, pair].rearrange("d (h c) t -> d h (c t)", c=KC),
                                         PART[w][:, parts[which], :]).then_inc(qk_in[pair], 16)
                t = seq(i, k, 2)
                if t:
                    sp.wait_ge(x2_ok, t.n(1, 1))
                    sp.nop(nofuse=True)
                    sp.dma_start(x2_seq[t.n()], x2[:, t.slot(2), :]).then_inc(x2_out[t.slot(2)], 16)
                t = seq(i, k, -3)
                if t:
                    if t.reached(4):
                        sp.wait_ge(tr_ready, t.n(4, -12))
                        sp.nop(nofuse=True)
                    for h in range(0, HEADS, 8):
                        sp.dma_start(sc[:, t.slot(4), h * P:(h + 8) * P].rearrange("p (h k) -> p h k", h=8),
                                     bias_seq[t.n(), :, h:h + 8, :]).then_inc(bias_in[t.slot(4)], 16)

            run_steps(sp, FIRST, LAST, U, LOOP, step)

            for q in x2_out:
                sp.wait_ge(q, 16 * (N // 2))
            sp.wait_ge(ids_out, 16 * N)
            sp.wait_ge(tab_ok, 1)

            def fstep(i, k):
                t = tile(i, k, -5)
                if t:
                    if t.reached(8):
                        sp.wait_ge(og_out[t.slot(2)], t.per(2, 16 * HALVES, -48 * HALVES))
                        sp.nop(nofuse=True)
                    b = sp.value_load(tile_b[0:1, bass.ds(t.n(), 1)], min_val=0, max_val=LIST - FT)
                    sp.dma_start(ids[:, t.slot(8), :],
                                 list_dram[bass.ds(b, FT), :].rearrange("(p a) o -> p (a o)", p=P)
                                 ).then_inc(ids_in[t.slot(8)], 16)
                t = tile(i, k, -2)
                if t:
                    if t.reached(4):
                        sp.wait_ge(y_ready, t.n(1, -3))
                        sp.nop(nofuse=True)
                    e = sp.value_load(tile_e[0:1, bass.ds(t.n(), 1)], min_val=0, max_val=EXPERTS - 1)
                    sp.dma_start(w1_sb[:, t.slot(4)], w1[e]).then_inc(w1_in[t.slot(4)], 16)
                    sp.dma_start(w2_sb[:, t.slot(4)], w2[e]).then_inc(w2_in[t.slot(4)], 16)
                    sp.dma_start(b2_sb[:, t.slot(4)], b2[bass.ds(e, 1), :]).then_inc(w2_in[t.slot(4)], 16)

            run_steps(sp, FFIRST, FLAST, FU, FLOOP, fstep)
            for q in og_out:
                sp.wait_ge(q, 16 * HALVES * TILES // 2)

        @block.gpsimd
        def _(pool):
            nc.gpsimd.memset(empty[:], NO_TOKEN).then_inc(s_setg, 1)
            nc.gpsimd.memset(V[:], 1.0).then_inc(s_setg, 1)
            pool.wait_ge(s_setd, 9)
            pool.wait_ge(s_list0, 16)

            def subtract_max(t, h):
                pool.wait_ge(max_ok, t.n(2, h + 1))
                s = sc[:, t.slot(4), 1024 * h:1024 * h + 1024].rearrange("p (h k) -> p h k", h=8)
                m = negmax[:, t.slot(2), 8 * h:8 * h + 8].unsqueeze(2).broadcast_to([P, 8, P])
                nc.gpsimd.tensor_tensor(s, s, m, ALU.add).then_inc(sub_ok, 1)

            def step(i, k):
                cur, late = seq(i, k, 0), seq(i, k, -2)
                if late and late.slot(2) == 0:
                    for n, w in enumerate("qk"):
                        pool.wait_ge(p0_ok, late.per(2, 2, n + 1))
                        if late.reached(2):
                            pool.wait_ge(p2_ok, late.per(2, 2))
                        nc.gpsimd.tensor_tensor(REST[w][:], F[w][:], PART[w][:, 0, :],
                                                ALU.subtract).then_inc(rest_ok, 1)
                if cur:
                    subtract_max(cur, 0)
                norms = norms_at(i, k)
                if norms:
                    a, b = norms
                    pool.wait_ge(ve_ok, At(i, k, U).n(1, 6))
                    nc.gpsimd.tensor_tensor(rs[:, a:b, 0], ve[:, a:b, 0], minus_half.broadcast_to([P, b - a]),
                                            ALU.pow).then_inc(rs_ok, 1)
                if late and late.slot(2) == 0:
                    for n, w in enumerate("qk"):
                        pool.wait_ge(p1_ok, late.per(2, 2, n + 1))
                        nc.gpsimd.tensor_tensor(PART[w][:, 2, :], REST[w][:], PART[w][:, 1, :],
                                                ALU.subtract).then_inc(p2_ok, 1)
                if cur:
                    subtract_max(cur, 1)
                t = seq(i, k, 6)
                if t and t.slot(4) == 3:
                    pool.wait_ge(slot_ok, t.per(4, 1, 1))
                    pool.nop(nofuse=True)
                    for j in range(4):
                        nc.gpsimd.indirect_dma_start(
                            list_dram, bass.IndirectOffsetOnAxis(ap=slot_i[:, j:j + 1], axis=0),
                            ids4_i[:, j:j + 1], None).then_inc(ids_out, 16)

            run_steps(pool, FIRST, LAST, U, LOOP, step)
            for q in x2_out:
                pool.wait_ge(q, 16 * (N // 2))

            def fstep(i, k):
                t = tile(i, k, -3)
                if t:
                    pool.wait_ge(idc_ok, t.n(1, 1))
                    if t.reached(8):
                        pool.wait_ge(og_ok, t.n(1, -7))
                    pool.nop(nofuse=True)
                    for a in range(HALVES):
                        nc.gpsimd.indirect_dma_start(
                            xg[:, t.slot(8), a, :], None, x2_dram,
                            bass.IndirectOffsetOnAxis(ap=idc[:, t.slot(4), a:a + 1], axis=0)
                        ).then_inc(xg_in[t.slot(8)], 16)
                t = tile(i, k, -2)
                if t:
                    pool.wait_ge(veg_ok, t.n(1, 1))
                    nc.gpsimd.tensor_tensor(rsg[:], veg[:], minus_half.broadcast_to([P, HALVES]),
                                            ALU.pow).then_inc(rsg_ok, 1)
                t = tile(i, k, 2)
                if t:
                    pool.wait_ge(og_ok, t.n(1, 1))
                    pool.nop(nofuse=True)
                    for a in range(HALVES):
                        nc.gpsimd.indirect_dma_start(
                            out_rows, bass.IndirectOffsetOnAxis(ap=ids[:, t.slot(8), a:a + 1], axis=0),
                            og[:, t.slot(2), a, :], None, bounds_check=TOKENS - 1, oob_is_err=False
                        ).then_inc(og_out[t.slot(2)], 16)

            run_steps(pool, FFIRST, FLAST, FU, FLOOP, fstep)

        @block.tensor
        def _(pe):
            mm = nc.tensor.matmul
            pe.wait_ge(s_set, 16 * SETUP_DMAS)
            for n, w in enumerate("qkv"):
                for c in range(KC):
                    ins = mm(bank[n][:, c * HID:(c + 1) * HID], A[w][:, c * P:(c + 1) * P], B[w][:],
                             start=True, stop=True)
            ins.then_inc(s_setp, 1)
            pe.wait_ge(s_setd, 9)

            def scores(t, q):
                pair, tok = t.k // 2 % 2, P * t.slot(2)
                if q == 0 and t.slot(2) == 0:
                    pe.wait_ge(qk_in[pair], t.per(4, 32 * len(PAIRS), 32 * len(PAIRS)))
                if q >= 2 or t.reached(1):
                    pe.wait_ge(s_used, t.n(4, q - 1))
                for h in range(4 * q, 4 * q + 4):
                    col = h % 8 * KC + h // 8
                    ins = mm(b_s[q % 2][:, P * (h % 4):P * (h % 4) + P], ST["q"][:, pair, col, tok:tok + P],
                             ST["k"][:, pair, col, tok:tok + P], start=True, stop=True)
                ins.then_inc(s_ready, 1)

            def turn(t, q):
                if q % 2 == 0:
                    pe.wait_ge(sub_ok, t.n(2, q // 2 + 1))
                if q >= 2 or t.reached(1):
                    pe.wait_ge(pt_ready, t.n(4, q - 1))
                for h in range(4):
                    o = 512 * q + P * h
                    ins = nc.tensor.transpose(b_t[q % 2][:, P * h:P * h + P], sc[:, t.slot(4), o:o + P], ident)
                ins.then_inc(tr_ready, 1)

            def step(i, k):
                nxt, cur, prev, fin, old, gate = (seq(i, k, lag) for lag in (-4, 0, 1, 2, 3, 4))
                here = At(i, k, U)
                if cur:
                    scores(cur, 0)
                if prev:
                    turn(prev, 0)
                if fin:
                    pe.wait_ge(pt_ready, fin.n(4, 4))
                    if fin.reached(1):
                        pe.wait_ge(ot_evac, fin.n())
                    pe.wait_ge(xt_evac, nxt.n() if nxt else N)
                    for h in range(HEADS):
                        j = h % 4
                        ins = mm(b_x[CELL * j:CELL * j + CELL, P * (h // 4):P * (h // 4) + P],
                                 V[:, fin.slot(8), h, :], PT[:, fin.slot(2), P * h:P * h + P],
                                 start=True, stop=True, tile_position=(0, CELL * j))
                    ins.then_inc(ot_ready, 1)
                if cur:
                    scores(cur, 1)
                if prev:
                    turn(prev, 1)
                ins = None
                if here.reached(3):
                    pe.wait_ge(o_used, here.n(1, -2))
                if fin:
                    pe.wait_ge(ot_evac, fin.n(1, 1))
                    for g in range(HEADS // 4):
                        ins = nc.tensor.transpose(b_o[:, P * g:P * g + P], OT[:, P * g:P * g + P], ident)
                if gate:
                    pe.wait_ge(x2t_evac, gate.n(1, 1))
                    for c in range(KC):
                        ins = mm(log_ps, x2T[:, gate.slot(2), c, :], wg_sb[:, c, :],
                                 start=(c == 0), stop=(c == KC - 1))
                grp = seq(i, k, 5)
                if grp and grp.slot(4) == 3:
                    pe.wait_ge(cnt_ok, grp.per(4, 4, 4))
                    mm(pos_ps, tri, OH[:], start=True, stop=False)
                    ins = mm(pos_ps, ones, CNT[:, 0:4, :], start=False, stop=True)
                if ins:
                    ins.then_inc(o_ready, 1)
                if nxt:
                    pe.wait_ge(xn_ok, nxt.n(1, 1))
                    pe.wait_ge(ctx_inn[nxt.slot(4)], nxt.per(4, 16, 16))
                    if nxt.reached(1):
                        pe.wait_ge(xt_evac, nxt.n())
                    if fin:
                        pe.wait_ge(ot_evac, fin.n(1, 1))
                    for c in range(KC):
                        nc.tensor.transpose(b_x[:, c * P:c * P + P],
                                            xn[:, nxt.slot(2), c * P:c * P + P], ident)
                    for c in range(KC):
                        ins = nc.tensor.transpose(b_x[:, (KC + c) * P:(KC + c) * P + P],
                                                  ctx_sb[:, nxt.slot(4), c * P:c * P + P], ident)
                    ins.then_inc(xt_ready, 1)
                if cur:
                    scores(cur, 2)
                if prev:
                    turn(prev, 2)
                if old:
                    pe.wait_ge(xn2_ok, old.n(1, 1))
                    if old.reached(1):
                        pe.wait_ge(x2t_evac, old.n())
                    pe.wait_ge(q_evac, nxt.per(2) if nxt else N // 2)
                    for c in range(KC):
                        ins = nc.tensor.transpose(b_q[:, c * P:c * P + P],
                                                  xn2[:, old.slot(2), c * P:c * P + P], ident)
                    ins.then_inc(x2t_ready, 1)
                if nxt:
                    pair, tok = nxt.k // 2 % 2, P * nxt.slot(2)
                    pe.wait_ge(xt_evac, nxt.n(1, 1))
                    if nxt.reached(1):
                        pe.wait_ge(v_evac, nxt.n())
                    if nxt.reached(2):
                        pe.wait_ge(k_evac, nxt.per(2))
                    mm(b_vk[:, 0:HID], ones[0:1, :], bv_row[:], start=True, stop=False)
                    for c in range(KC):
                        ins = mm(b_vk[:, 0:HID], XT[:, pair, KC + c, tok:tok + P], W["v"][:, c, :],
                                 start=False, stop=(c == KC - 1))
                    ins.then_inc(v_ready, 1)
                if cur:
                    scores(cur, 3)
                if prev:
                    turn(prev, 3)
                if nxt and nxt.slot(2) == 1:
                    if nxt.reached(2):
                        pe.wait_ge(q_evac, nxt.per(2))
                    if old:
                        pe.wait_ge(x2t_evac, old.n(1, 1))
                    for o in range(KC):
                        for c in range(KC):
                            ins = mm(b_q[:, 256 * o:256 * o + 256], W["q"][:, c, o * P:o * P + P],
                                     XT[:, pair, c, :], start=(c == 0), stop=(c == KC - 1))
                    ins.then_inc(q_ready, 1)
                    pe.wait_ge(v_evac, nxt.n(1, 1))
                    for o in range(KC):
                        for c in range(KC):
                            ins = mm(b_vk[:, 256 * o:256 * o + 256], W["k"][:, c, o * P:o * P + P],
                                     XT[:, pair, KC + c, :], start=(c == 0), stop=(c == KC - 1))
                    ins.then_inc(k_ready, 1)

            run_steps(pe, FIRST, LAST, U, LOOP, step)

            pe.wait_ge(o_used, N + 3)
            mm(b_o[:, 0:EXPERTS], ones, CNT[:, 4, :], start=True, stop=True).then_inc(c_ready, 1)

            def fstep(i, k):
                t = tile(i, k, 0)
                if t:
                    pe.wait_ge(gt_evac, t.n(1, 1))
                    pe.wait_ge(w1_in[t.slot(4)], t.per(4, 16, 16))
                    if t.reached(2):
                        pe.wait_ge(h_ok, t.n(1, -1))
                    for o in range(KC):
                        for c in range(KC):
                            ins = mm(bank[2 + t.slot(2)][:, FT * o:FT * o + FT],
                                     w1_sb[:, t.slot(4), c * HID + o * P:c * HID + o * P + P],
                                     xgT[:, t.slot(2), c, :], start=(c == 0), stop=(c == KC - 1))
                    ins.then_inc(h_ready, 1)
                t = tile(i, k, 1)
                if t:
                    pe.wait_ge(h_ok, t.n(1, 1))
                    pe.wait_ge(w2_in[t.slot(4)], t.per(4, 32, 32))
                    if t.reached(2):
                        pe.wait_ge(og_ok, t.n(1, -1))
                    for a in range(HALVES):
                        y_half = bank[6 + t.slot(2)][:, HID * a:HID * a + HID]
                        mm(y_half, ones[0:1, :], b2_sb[:, t.slot(4), :], start=True, stop=False)
                        for c in range(KC):
                            ins = mm(y_half, hT[:, t.slot(2), c, a * P:a * P + P],
                                     w2_sb[:, t.slot(4), c * HID:c * HID + HID], start=False, stop=(c == KC - 1))
                    ins.then_inc(y_ready, 1)
                t = tile(i, k, -1)
                if t:
                    pe.wait_ge(xgn_ok, t.n(HALVES, HALVES))
                    if t.reached(2):
                        pe.wait_ge(gt_evac, t.n(1, -1))
                    for c in range(KC):
                        for a in range(HALVES):
                            o = c * FT + a * P
                            ins = nc.tensor.transpose(bank[t.slot(2)][:, o:o + P],
                                                      xgn[:, t.slot(2), a, c * P:c * P + P], ident)
                    ins.then_inc(gt_ready, 1)

            run_steps(pe, FFIRST, FLAST, FU, FLOOP, fstep)

        @block.scalar
        def _(act):
            act.wait_ge(s_set, 16 * SETUP_DMAS)
            nc.scalar.activation(tg[:], g_raw[:], ACT.Tanh).then_inc(s_seta, 1)
            act.wait_ge(s_setd, 9)
            act.wait_ge(s_setg, 2)

            def step(i, k):
                nxt, late, prev, fin, old = (seq(i, k, lag) for lag in (-4, -2, 1, 2, 3))

                def probs(q):
                    act.wait_ge(tr_ready, prev.n(4, q + 1))
                    if q == 0 and prev.reached(2):
                        act.wait_ge(ot_ready, prev.n(1, -1))
                    nc.scalar.activation(PT[:, prev.slot(2), 512 * q:512 * q + 512], b_t[q % 2][:],
                                         ACT.Exp).then_inc(pt_ready, 1)

                if prev:
                    probs(0)
                if fin:
                    act.wait_ge(ot_ready, fin.n(1, 1))
                    if fin.reached(1):
                        act.wait_ge(o_ready, fin.n())
                    nc.scalar.copy(OT[:], b_x[:]).then_inc(ot_evac, 1)
                if prev:
                    probs(1)
                if nxt:
                    pair, tok = nxt.k // 2 % 2, P * nxt.slot(2)
                    act.wait_ge(xt_ready, nxt.n(1, 1))
                    if nxt.reached(4):
                        act.wait_ge(k_ready, nxt.per(2, 1, -1))
                    nc.scalar.copy(XT[:, pair, :, tok:tok + P],
                                   b_x[:].rearrange("p (c t) -> p c t", t=P)).then_inc(xt_evac, 1)
                if late and late.slot(2) == 0:
                    for n, w in enumerate("qk"):
                        act.wait_ge(rest_ok, late.per(2, 2, n + 1))
                        nc.scalar.copy(PART[w][:, 1, :], REST[w][:]).then_inc(p1_ok, 1)
                if prev:
                    probs(2)
                if old:
                    act.wait_ge(x2t_ready, old.n(1, 1))
                    if old.reached(2):
                        act.wait_ge(o_ready, old.n(1, 1))
                    nc.scalar.copy(x2T[:, old.slot(2)], b_q[:, 0:HID].rearrange("p (c t) -> p c t", t=P)
                                   ).then_inc(x2t_evac, 1)
                if nxt:
                    act.wait_ge(v_ready, nxt.n(1, 1))
                    if nxt.reached(8):
                        act.wait_ge(ot_ready, nxt.n(1, -7))
                    nc.scalar.copy(V[:, nxt.slot(8), :, 0:D],
                                   b_vk[:, 0:HID].rearrange("p (h d) -> p h d", d=D)).then_inc(v_evac, 1)
                if prev:
                    probs(3)
                if nxt and nxt.slot(2) == 1:
                    for n, (w, ps, ready, evac, col) in enumerate((("q", b_q, q_ready, q_evac, bq_col),
                                                                   ("k", b_vk, k_ready, k_evac, bk_col))):
                        act.wait_ge(ready, nxt.per(2, 1, 1))
                        if nxt.reached(2):
                            act.wait_ge(rest_ok, nxt.per(2, 2))
                            act.wait_ge(qk_in[(nxt.k // 2 + 1) % 2],
                                        nxt.minus(2).per(4, 32 * len(PAIRS), 32 * len(PAIRS)))
                        for o in range(KC):
                            ins = nc.scalar.activation(F[w][:, 256 * o:256 * o + 256],
                                                       ps[:, 256 * o:256 * o + 256],
                                                       ACT.Identity, bias=col[:, o:o + 1])
                        ins.then_inc(evac, 1)
                        act.wait_ge(evac, nxt.per(2, 1, 1))
                        nc.scalar.copy(PART[w][:, 0, :], F[w][:]).then_inc(p0_ok, 1)

            run_steps(act, FIRST, LAST, U, LOOP, step)

            def fstep(i, k):
                t = tile(i, k, 0)
                if t:
                    act.wait_ge(h_ready, t.n(1, 1))
                    if t.reached(2):
                        act.wait_ge(y_ready, t.n(1, -1))
                    for o in range(KC):
                        ins = nc.scalar.activation(hT[:, t.slot(2), o, :],
                                                   bank[2 + t.slot(2)][:, FT * o:FT * o + FT], ACT.Gelu,
                                                   bias=w1_sb[:, t.slot(4), KC * HID + o:KC * HID + o + 1])
                    ins.then_inc(h_ok, 1)
                t = tile(i, k, -1)
                if t:
                    act.wait_ge(gt_ready, t.n(1, 1))
                    if t.reached(2):
                        act.wait_ge(h_ready, t.n(1, -1))
                    nc.scalar.copy(xgT[:, t.slot(2)], bank[t.slot(2)][:].rearrange("p (c t) -> p c t", t=FT)
                                   ).then_inc(gt_evac, 1)

            run_steps(act, FFIRST, FLAST, FU, FLOOP, fstep)

        @block.vector
        def _(dve):
            dve.wait_ge(s_set, 16 * SETUP_DMAS)
            dve.wait_ge(s_setp, 1)
            dve.wait_ge(s_seta, 1)
            for n, w in enumerate("qkv"):
                nc.vector.scalar_tensor_tensor(out=W[w][:], in0=bank[n][:].rearrange("p (c h) -> p c h", c=KC),
                                               scalar=LORA, in1=W[w][:], op0=ALU.mult, op1=ALU.add).then_inc(s_setd, 1)
            nc.vector.memset(CNT[:], 0.0).then_inc(s_setd, 1)
            nc.vector.memset(zero8[:], 0.0).then_inc(s_setd, 1)
            dve.wait_ge(s_setd, 5)
            nc.vector.tensor_scalar(W["q"][:], W["q"][:], D ** -0.5, None, ALU.mult).then_inc(s_setd, 1)
            nc.vector.tensor_scalar(bq_col[:], bq_col[:], D ** -0.5, None, ALU.mult).then_inc(s_setd, 1)
            nc.vector.tensor_scalar(W["v"][:], W["v"][:], tg[:, 0:1], None, ALU.mult).then_inc(s_setd, 1)
            nc.vector.tensor_scalar(bv_row[:], bv_row[:], tg[0:1, 0:1], None, ALU.mult).then_inc(s_setd, 1)
            dve.wait_ge(s_setd, 9)

            def row_apply(src, dst, mv, rs, rs_s, done, at, free=None):
                dve.wait_ge(rs_s, at)
                if free:
                    dve.wait_ge(*free)
                nc.vector.tensor_scalar(dst, src, mv[:, 0:1], rs, ALU.subtract, ALU.mult).then_inc(done, 1)

            def add_bias(t, q):
                if q == 0:
                    dve.wait_ge(bias_in[t.slot(4)], t.per(4, 32, 32))
                dve.wait_ge(s_ready, t.n(4, q + 1))
                s = sc[:, t.slot(4), 512 * q:512 * q + 512]
                nc.vector.tensor_tensor(s, b_s[q % 2][:], s, ALU.add).then_inc(s_used, 1)

            def row_max(t, h):
                dve.wait_ge(s_used, t.n(4, 2 * h + 2))
                if h == 0 and t.reached(2):
                    dve.wait_ge(sub_ok, t.n(2, -2))
                nc.vector.tensor_reduce(
                    negmax[:, t.slot(2), 8 * h:8 * h + 8],
                    sc[:, t.slot(4), 1024 * h:1024 * h + 1024].rearrange("p (h k) -> p h k", h=8),
                    AX.X, ALU.max, negate=True).then_inc(max_ok, 1)

            def step(i, k):
                cur, done, gate, ahead = seq(i, k, 0), seq(i, k, 2), seq(i, k, 4), seq(i, k, -5)
                here = At(i, k, U)
                if cur:
                    add_bias(cur, 0)
                    add_bias(cur, 1)
                    row_max(cur, 0)
                if here.reached(2) and (gate or done or seq(i, k, 5)):
                    dve.wait_ge(o_ready, here.n(1, -1))
                    if gate:
                        if gate.slot(4) == 0 and gate.reached(4):
                            dve.wait_ge(oh_ok, gate.per(4))
                        ins = nc.vector.tensor_tensor(L[:, gate.slot(4), :], log_ps, bg_all[:], ALU.add)
                        ins.then_inc(l_ok, 1)
                    grp = seq(i, k, 5)
                    if grp and grp.slot(4) == 3:
                        g = grp.per(4, 1, 1)
                        if grp.reached(7):
                            dve.wait_ge(ids4_next, grp.per(4))
                        ins = nc.vector.tensor_tensor(where[:], pos_ps, ebase, ALU.add)
                        ins.then_inc(pos_ok, 1)
                        dve.wait_ge(pos_ok, g)
                        nc.vector.tensor_tensor(where[:], where[:], OH[:], ALU.mult).then_inc(where_ok, 1)
                        dve.wait_ge(where_ok, g)
                        nc.vector.tensor_reduce(slot_f[:], where[:], AX.X, ALU.add).then_inc(slotf_ok, 1)
                        dve.wait_ge(slotf_ok, g)
                        if grp.reached(7):
                            dve.wait_ge(ids_out, grp.per(4, 64))
                        nc.vector.tensor_copy(ids4_i[:], ids4[:]).then_inc(ids4_ok, 1)
                        nc.vector.tensor_copy(slot_i[:], slot_f[:]).then_inc(slot_ok, 1)
                        dve.wait_ge(ids4_ok, g)
                        nc.vector.tensor_scalar(ids4[:], ids4[:], float(4 * P), None, ALU.add).then_inc(ids4_next, 1)
                    if done:
                        nc.vector.reciprocal(rden[:], o_ps[:, :, D]).then_inc(rden_ok, 1)
                        dve.wait_ge(rden_ok, done.n(1, 1))
                        if done.reached(2):
                            dve.wait_ge(x2_out[done.slot(2)], done.per(2, 16))
                        y = x2[:, done.slot(2), :]
                        nc.vector.tensor_tensor(y.rearrange("p (h d) -> p h d", d=D), o_ps[:, :, 0:D],
                                                rden[:].unsqueeze(2).broadcast_to([P, HEADS, D]),
                                                ALU.mult).then_inc(o_used, 1)
                        dve.wait_ge(o_used, here.n(1, -1))
                        nc.vector.tensor_tensor(y, y, x_sb[:, done.slot(8), :], ALU.add).then_inc(x2_ok, 1)
                    else:
                        if gate:
                            dve.wait_ge(l_ok, gate.n(1, 1))
                        dve.sem_inc(o_used, 1)
                norms = []
                if ahead:
                    norms.append((0, ahead, x_sb[:, ahead.slot(8), :]))
                    dve.wait_ge(x_in[ahead.slot(8)], ahead.per(8, 16, 16))
                if done:
                    norms.append((1, done, x2[:, done.slot(2), :]))
                for n, t, rows in norms:
                    if n:
                        dve.wait_ge(x2_ok, t.n(1, 1))
                    nc.vector.bn_stats(st[:, n, :], rows).then_inc(st_ok[n], 1)
                for n, t, rows in norms:
                    dve.wait_ge(st_ok[n], t.n(1, 1))
                    dve.nop(nofuse=True)
                    nc.vector.bn_aggr(mv[:, n, :], st[:, n, :]).then_inc(mv_ok[n], 1)
                for n, t, rows in norms:
                    dve.wait_ge(mv_ok[n], t.n(1, 1))
                if norms:
                    a, b = norms_at(i, k)
                    nc.vector.tensor_scalar(ve[:, a:b, 0], mv[:, a:b, 1], EPS, None, ALU.add).then_inc(ve_ok, 1)
                if cur:
                    add_bias(cur, 2)
                    add_bias(cur, 3)
                    row_max(cur, 1)
                for n, t, rows in norms:
                    dst, done_ok, turned = ((xn, xn_ok, xt_ready), (xn2, xn2_ok, x2t_ready))[n]
                    row_apply(rows, dst[:, t.slot(2), :], mv[:, n, :], rs[:, n, :], rs_ok, done_ok, here.n(1, 6),
                              (turned, t.n(1, -1)) if t.reached(2) else None)
                if gate and gate.slot(4) == 3:
                    g = gate.per(4, 1, 1)
                    dve.wait_ge(l_ok, gate.n(1, 1))
                    nc.vector.tensor_reduce(lmax[:], L[:], AX.X, ALU.max).then_inc(lmax_ok, 1)
                    dve.wait_ge(lmax_ok, g)
                    nc.vector.tensor_tensor(key[:], L[:], lmax[:].unsqueeze(2).broadcast_to([P, 4, EXPERTS]),
                                            ALU.is_lt).then_inc(lt_ok, 1)
                    dve.wait_ge(lt_ok, g)
                    nc.vector.scalar_tensor_tensor(out=key[:], in0=key[:], scalar=float(2 * EXPERTS), in1=iota,
                                                   op0=ALU.mult, op1=ALU.add).then_inc(key_ok, 1)
                    dve.wait_ge(key_ok, g)
                    nc.vector.tensor_reduce(pick[:], key[:], AX.X, ALU.min).then_inc(pick_ok, 1)
                    dve.wait_ge(pick_ok, g)
                    nc.vector.tensor_tensor(OH[:], iota, pick[:].unsqueeze(2).broadcast_to([P, 4, EXPERTS]),
                                            ALU.is_equal).then_inc(oh_ok, 1)
                    nc.vector.tensor_copy(CNT[:, 0, :], CNT[:, 4, :]).then_inc(cnt0_ok, 1)
                    dve.wait_ge(oh_ok, g)
                    dve.wait_ge(cnt0_ok, g)
                    for j in range(4):
                        nc.vector.tensor_tensor(CNT[:, j + 1, :], CNT[:, j, :], OH[:, j, :], ALU.add).then_inc(cnt_ok, 1)
                        dve.wait_ge(cnt_ok, gate.per(4, 4, j + 1))

            run_steps(dve, FIRST, LAST, U, LOOP, step)

            made = [0]

            def link(ins):
                made[0] += 1
                ins.then_inc(s_tab, 1)
                dve.wait_ge(s_tab, made[0])

            M = TOKENS // FT
            dve.wait_ge(c_ready, 1)
            link(nc.vector.tensor_copy(cnt[:], b_o[0:1, 0:EXPERTS]))
            link(nc.vector.tensor_tensor(over[:], cnt[:].unsqueeze(2).broadcast_to([1, EXPERTS, M]),
                                         row[:, R_M:R_J].rearrange("p (e m) -> p e m", m=M), ALU.is_gt))
            link(nc.vector.tensor_reduce(nt[:], over[:], AX.X, ALU.add))
            link(nc.vector.tensor_tensor_scan(end[:], nt[:], zero8[:], 0.0, ALU.add, ALU.add))
            link(nc.vector.tensor_tensor(past[:], row[:, R_J:R_J256].rearrange("p (j e) -> p j e", e=EXPERTS),
                                         end[:].unsqueeze(1).broadcast_to([1, TILES, EXPERTS]), ALU.is_ge))
            link(nc.vector.tensor_tensor(ptn[:], past[:], nt[:].unsqueeze(1).broadcast_to([1, TILES, EXPERTS]),
                                         ALU.mult))
            link(nc.vector.tensor_reduce(e_f[:], past[:], AX.X, ALU.add))
            link(nc.vector.tensor_reduce(s_f[:], ptn[:], AX.X, ALU.add))
            link(nc.vector.scalar_tensor_tensor(out=b_f[:], in0=s_f[:], scalar=float(-FT), in1=row[:, R_J256:R_END],
                                                op0=ALU.mult, op1=ALU.add))
            link(nc.vector.scalar_tensor_tensor(out=b_f[:], in0=e_f[:], scalar=float(TOKENS), in1=b_f[:],
                                                op0=ALU.mult, op1=ALU.add))
            link(nc.vector.tensor_scalar(ec_f[:], e_f[:], float(EXPERTS - 1), None, ALU.min))
            link(nc.vector.tensor_copy(tile_e[:], ec_f[:]))
            nc.vector.tensor_copy(tile_b[:], b_f[:]).then_inc(tab_ok, 1)

            def fstep(i, k):
                t = tile(i, k, -4)
                if t:
                    dve.wait_ge(ids_in[t.slot(8)], t.per(8, 16, 16))
                    if t.reached(4):
                        dve.wait_ge(xg_in[(t.k + 4) % 8], t.minus(4).per(8, 32, 32))
                    nc.vector.tensor_scalar(idc[:, t.slot(4), :], ids[:, t.slot(8), :], float(TOKENS - 1), None,
                                            ALU.min).then_inc(idc_ok, 1)
                t = tile(i, k, -1)
                if t:
                    for a in range(HALVES):
                        row_apply(xg[:, t.slot(8), a, :], xgn[:, t.slot(2), a, :], mvg[:, a, :], rsg[:, a:a + 1],
                                  rsg_ok, xgn_ok, t.n(1, 1),
                                  (gt_ready, t.n(1, -1)) if a == 0 and t.reached(2) else None)
                t = tile(i, k, 2)
                if t:
                    dve.wait_ge(y_ready, t.n(1, 1))
                    if t.reached(2):
                        dve.wait_ge(og_out[t.slot(2)], t.per(2, 16 * HALVES))
                    nc.vector.scalar_tensor_tensor(out=og[:, t.slot(2)].rearrange("p a h -> p (a h)"),
                                                   in0=bank[6 + t.slot(2)][:], scalar=tg[:, 1:2],
                                                   in1=xg[:, t.slot(8)].rearrange("p a h -> p (a h)"),
                                                   op0=ALU.mult, op1=ALU.add).then_inc(og_ok, 1)
                t = tile(i, k, -2)
                if t:
                    dve.wait_ge(xg_in[t.slot(8)], t.per(8, 32, 32))
                    for a in range(HALVES):
                        nc.vector.bn_stats(stg[:, a, :], xg[:, t.slot(8), a, :]).then_inc(stg_ok, 1)
                    for a in range(HALVES):
                        dve.wait_ge(stg_ok, t.n(HALVES, a + 1))
                        dve.nop(nofuse=True)
                        nc.vector.bn_aggr(mvg[:, a, :], stg[:, a, :]).then_inc(mvg_ok, 1)
                    dve.wait_ge(mvg_ok, t.n(HALVES, HALVES))
                    nc.vector.tensor_scalar(veg[:], mvg[:, :, 1], EPS, None, ALU.add).then_inc(veg_ok, 1)

            run_steps(dve, FFIRST, FLAST, FU, FLOOP, fstep)


def kernel(**inputs):
    import numpy as np
    import concourse.bacc as bacc
    from concourse.bass_utils import run_bass_kernel_spmd

    a = {k: np.ascontiguousarray(v) for k, v in inputs.items()}

    def chunks(m):
        return np.ascontiguousarray(m.reshape(KC, P, -1).transpose(1, 0, 2))

    arrays = {
        "x": a["x"], "ctx_in": a["ctx_1024"], "bias": a["fside_Bx16xSxS2_0"],
        "g_xattn": a["g_xattn"].reshape(1), "g_ffn": a["g_ffn"].reshape(1),
    }
    def heads_inside(m):
        return np.ascontiguousarray(m.reshape(-1, KC, 8, D).transpose(0, 1, 3, 2).reshape(-1, HID))

    for w in "qkv":
        wt, b, bt = a[f"L0_xattn_W{w}"].T, a[f"L0_xattn_b{w}"], a[f"L0_xattn_B{w}"].T
        if w != "v":
            wt, b, bt = heads_inside(wt), np.ascontiguousarray(heads_inside(b).reshape(KC, P).T), heads_inside(bt)
        b = b.reshape(1, HID) if w == "v" else b
        arrays[f"w{w}T"], arrays[f"b{w}"], arrays[f"b{w}T"] = chunks(wt), b, np.ascontiguousarray(bt)
        arrays[f"a{w}"] = a[f"L0_xattn_A{w}"]
    arrays["wg"] = chunks(a["L0_ffn_Wg"])
    arrays["bg"] = a["L0_ffn_bg"].reshape(1, EXPERTS)
    w1 = np.stack([chunks(m).reshape(P, KC * HID) for m in a["L0_ffn_W1"]])
    b1 = a["L0_ffn_b1"].reshape(EXPERTS, KC, P).transpose(0, 2, 1)
    arrays["w1"] = np.ascontiguousarray(np.concatenate([w1, b1], axis=2))
    arrays["w2"] = np.stack([chunks(m).reshape(P, KC * HID) for m in a["L0_ffn_W2"]])
    arrays["b2"] = a["L0_ffn_b2"]

    c = np.zeros((P, C_END), np.float32)
    c[:, C_ID:C_ID + P] = np.eye(P)
    c[:, C_TRI:C_TRI + P] = np.triu(np.ones((P, P)), 1)
    c[:, C_ONE:C_ONE + P] = 1
    c[:, C_HALF] = -0.5
    c[:, C_IOTA:C_IOTA + 32] = np.tile(np.arange(EXPERTS), 4)
    c[:, C_BASE:C_BASE + 32] = np.tile(np.arange(EXPERTS) * TOKENS, 4)
    r = np.zeros((1, R_END), np.float32)
    r[0, R_M:R_J] = np.tile(np.arange(TOKENS // FT) * FT, EXPERTS)
    r[0, R_J:R_J256] = np.repeat(np.arange(TILES), EXPERTS)
    r[0, R_J256:R_END] = np.arange(TILES) * FT
    arrays["consts"], arrays["row_consts"] = c, r
    arrays["ids_const"] = (np.arange(P)[:, None] + P * np.arange(4)[None, :]).astype(np.float32)

    nc = bacc.Bacc("TRN2", target_bir_lowering=False, num_devices=1)
    order = ["x", "ctx_in", "bias", "g_xattn", "g_ffn", "wqT", "bq", "aq", "bqT", "wkT", "bk", "ak", "bkT",
             "wvT", "bv", "av", "bvT", "wg", "bg", "w1", "w2", "b2", "consts", "row_consts", "ids_const"]
    aps = [nc.dram_tensor(f"in_{n}", arrays[n].shape, mybir.dt.from_np(arrays[n].dtype), kind="ExternalInput").ap()
           for n in order]
    out = nc.dram_tensor("out_0", (N, P, HID), F32, kind="ExternalOutput").ap()
    flamingo_block(nc, *aps, out)
    r = run_bass_kernel_spmd(nc, [{f"in_{n}": arrays[n] for n in order}], core_ids=[0])
    return r.results[0]["out_0"]
```

```python
from contextlib import ExitStack

import concourse.bass as bass
from concourse import mybir

F32 = mybir.dt.float32
I32 = mybir.dt.int32
BF16 = mybir.dt.bfloat16
ALU = mybir.AluOpType
ACT = mybir.ActivationFunctionType
AX = mybir.AxisListType

P = 128
N = 128
HID = 256
KC = HID // P
HEADS = 16
D = HID // HEADS
RANK = 8
LORA = 16.0 / RANK
EXPERTS = 8
EPS = 1e-5
TOKENS = N * P
U = 8

FT = 256
HALVES = FT // P
TILES = 72
FU = 8
NO_TOKEN = 1 << 20
LIST = EXPERTS * TOKENS + TILES * FT

PAIRS = [(0, 0), (0, 1), (0, 2), (1, 0), (1, 1), (2, 0)]
ROWS = D * len(PAIRS)
CELL = 32

C_ID, C_TRI, C_ONE, C_IOTA, C_BASE = 0, 128, 256, 384, 416
C_HALF = 448
C_END = 449
R_M, R_J, R_J256 = 0, EXPERTS * (TOKENS // FT), EXPERTS * (TOKENS // FT) + TILES * EXPERTS
R_END = R_J256 + TILES


class At:

    def __init__(self, i, k, width):
        self.i, self.k, self.width = i, k, width

    def slot(self, m):
        return self.k % m

    def n(self, mul=1, add=0):
        v = self.k * mul + add
        return self.i * (self.width * mul) + v

    def per(self, m, mul=1, add=0):
        v = (self.k // m) * mul + add
        return self.i * (self.width // m * mul) + v

    def minus(self, lag):
        return At(self.i, self.k - lag, self.width)

    def reached(self, least):
        return not isinstance(self.i, int) or self.i * self.width + self.k >= least




def run_steps(eng, first, last, width, loop_rounds, body):
    a, b = loop_rounds
    for s in range(first, a * width):
        body(0, s)
    with eng.Fori(a, b) as i:
        for k in range(width):
            body(i, k)
    for s in range(b * width, last + 1):
        body(0, s)


def flamingo_block(nc, x, ctx_in, bias, g_xattn, g_ffn, wqT, bq, aq, bqT, wkT, bk, ak, bkT, wvT, bv, av, bvT,
                   wg, bg, w1, w2, b2, consts, row_consts, ids_const, out):
    ctx = ExitStack()
    with ctx:
        def sb(name, shape, dt=F32):
            return ctx.enter_context(nc.sbuf_tensor(name, shape, dt))

        def sem(name):
            return ctx.enter_context(nc.semaphore(name))

        x2_dram = nc.dram_tensor("x2_dram", (TOKENS, HID), F32, kind="Internal").ap()
        list_dram = nc.dram_tensor("list_dram", (LIST, 1), I32, kind="Internal").ap()

        cst = sb("cst", [P, C_END])
        row = sb("row", [1, R_END])
        ids4 = sb("ids4", [P, 4])
        ids4_i = sb("ids4_i", [P, 2, 4], I32)
        empty = sb("empty", [P, LIST // P], I32)
        ident, tri, ones = cst[:, C_ID:C_ID + P], cst[:, C_TRI:C_TRI + P], cst[:, C_ONE:C_ONE + P]
        minus_half = cst[:, C_HALF:C_HALF + 1]
        iota = cst[:, C_IOTA:C_IOTA + 32].rearrange("p (j e) -> p j e", e=EXPERTS)
        ebase = cst[:, C_BASE:C_BASE + 32].rearrange("p (j e) -> p j e", e=EXPERTS)
        W = {w: sb(f"w{w}", [P, KC, HID]) for w in "qkv"}
        A = {w: sb(f"a{w}", [RANK, HID]) for w in "qkv"}
        B = {w: sb(f"b{w}", [RANK, HID]) for w in "qkv"}
        bq_col = sb("bq_col", [P, KC])
        bk_col = sb("bk_col", [P, KC])
        bv_row, bv_rest = sb("bv_row", [1, HID]), sb("bv_rest", [1, HID])
        bv_parts = sb("bv_parts", [1, 3, HID], BF16)
        bv_rows = sb("bv_rows", [3, HID], BF16)
        ones3 = sb("ones3", [3, P], BF16)
        bg_all = sb("bg_all", [P, EXPERTS])
        wg_sb = sb("wg_sb", [P, KC, EXPERTS])
        g_raw = sb("g_raw", [P, 2])
        tg = sb("tg", [P, 2])

        x_sb = sb("x_sb", [P, 8, HID])
        ctx_sb = sb("ctx_sb", [P, 4, HID])
        sc = sb("sc", [P, 4, HEADS * P])
        xn = sb("xn", [P, 2, HID])
        XT = sb("XT", [P, 2, 2 * KC, 2 * P])
        F = {w: sb(f"f{w}", [P, KC * 2 * P]) for w in "qk"}
        REST = {w: sb(f"rest{w}", [P, KC * 2 * P]) for w in "qk"}
        PART = {w: sb(f"part{w}", [P, 3, KC * 2 * P], BF16) for w in "qk"}
        ST = {w: sb(f"st{w}", [ROWS, 2, HEADS, 2 * P], BF16) for w in "qk"}
        V = sb("V", [P, 8, HEADS, CELL])
        PT = sb("PT", [P, 2, HEADS * P])
        OT = sb("OT", [P, HEADS // 4 * P])
        negmax = sb("negmax", [P, 2, HEADS])
        rden = sb("rden", [P, HEADS])
        x2 = sb("x2", [P, 2, HID])
        xn2 = sb("xn2", [P, 2, HID])
        x2T = sb("x2T", [P, 2, KC, P])
        st, mv = sb("st", [P, 2, 6]), sb("mv", [P, 2, 2])
        ve, rs, shift = sb("ve", [P, 2, 1]), sb("rs", [P, 2, 1]), sb("shift", [P, 2, 1])
        L = sb("L", [P, 4, EXPERTS])
        lmax, key, pick = sb("lmax", [P, 4]), sb("key", [P, 4, EXPERTS]), sb("pick", [P, 4])
        OH = sb("OH", [P, 4, EXPERTS])
        CNT = sb("CNT", [P, 5, EXPERTS])
        where = sb("where", [P, 4, EXPERTS])
        slot_f = sb("slot_f", [P, 4])
        slot_i = sb("slot_i", [P, 2, 4], I32)

        cnt = sb("cnt", [1, EXPERTS])
        over = sb("over", [1, EXPERTS, TOKENS // FT])
        nt = sb("nt", [1, EXPERTS])
        zero8 = sb("zero8", [1, EXPERTS])
        end = sb("end", [1, EXPERTS])
        past = sb("past", [1, TILES, EXPERTS])
        ptn = sb("ptn", [1, TILES, EXPERTS])
        e_f, s_f, b_f, ec_f = (sb(t, [1, TILES]) for t in ("e_f", "s_f", "b_f", "ec_f"))
        tile_e = sb("tile_e", [1, TILES], I32)
        tile_b = sb("tile_b", [1, TILES], I32)
        ids = sb("ids", [P, 8, HALVES], I32)
        idc = sb("idc", [P, 4, HALVES], I32)
        old_sc = sc[:].rearrange("p s c -> p (s c)")
        xg = old_sc[:, 0:8 * FT * KC].rearrange("p (s a h) -> p s a h", s=8, a=HALVES)
        w2_sb = old_sc[:, 8 * FT * KC:12 * FT * KC].rearrange("p (s w) -> p s w", s=4)
        xgn = sb("xgn", [P, 2, HALVES, HID])
        xgT = sb("xgT", [P, 2, KC, FT])
        hT = sb("hT", [P, 2, KC, FT])
        w1_sb = sb("w1_sb", [P, 4, KC * HID + KC])
        b2_sb = sb("b2_sb", [1, 4, HID])
        stg, mvg = sb("stg", [P, HALVES, 6]), sb("mvg", [P, HALVES, 2])
        veg, rsg = sb("veg", [P, HALVES]), sb("rsg", [P, HALVES])
        og = sb("og", [P, 2, HALVES, HID])

        bank = [ctx.enter_context(nc.psum_tensor(f"bank{i}", [P, 512], F32)) for i in range(8)]
        b_s, b_t = bank[0:2], bank[2:4]
        b_o, b_x, b_vk, b_q = bank[4], bank[5], bank[6], bank[7]
        o_ps = b_o[:].rearrange("p (h c) -> p h c", c=CELL)
        log_ps = o_ps[:, 0, D + 4:D + 4 + EXPERTS]
        pos_ps = o_ps[:, 1:HEADS:4, D + 4:D + 4 + EXPERTS]

        s_set = sem("s_set")
        s_bv, bv_in = sem("s_bv"), sem("bv_in")
        s_list0 = sem("s_list0")
        s_setp, s_setd, s_seta, s_setg = sem("s_setp"), sem("s_setd"), sem("s_seta"), sem("s_setg")
        x_in = [sem(f"x_in{i}") for i in range(8)]
        ctx_inn = [sem(f"ctx_in{i}") for i in range(4)]
        bias_in = [sem(f"bias_in{i}") for i in range(4)]
        st_ok, mv_ok = [sem(f"st_ok{i}") for i in range(2)], [sem(f"mv_ok{i}") for i in range(2)]
        ve_ok, rs_ok, shift_ok, xn_ok, xn2_ok = (sem(t) for t in ("ve_ok", "rs_ok", "shift_ok", "xn_ok", "xn2_ok"))
        xt_ready, xt_evac = sem("xt_ready"), sem("xt_evac")
        v_ready, v_evac = sem("v_ready"), sem("v_evac")
        q_ready, q_evac, k_ready, k_evac = sem("q_ready"), sem("q_evac"), sem("k_ready"), sem("k_evac")
        p0_ok, p1_ok, rest_ok, p2_ok = sem("p0_ok"), sem("p1_ok"), sem("rest_ok"), sem("p2_ok")
        qk_in = [sem(f"qk_in{i}") for i in range(2)]
        s_ready, s_used, max_ok, sub_ok = sem("s_ready"), sem("s_used"), sem("max_ok"), sem("sub_ok")
        tr_ready, pt_ready = sem("tr_ready"), sem("pt_ready")
        o_ready, o_used = sem("o_ready"), sem("o_used")
        ot_ready, ot_evac = sem("ot_ready"), sem("ot_evac")
        rden_ok, x2_ok = sem("rden_ok"), sem("x2_ok")
        x2_out = [sem(f"x2_out{i}") for i in range(2)]
        x2t_ready, x2t_evac = sem("x2t_ready"), sem("x2t_evac")
        l_ok, lmax_ok, lt_ok, key_ok, pick_ok, oh_ok, cnt0_ok, cnt_ok = (
            sem(t) for t in ("l_ok", "lmax_ok", "lt_ok", "key_ok", "pick_ok", "oh_ok", "cnt0_ok", "cnt_ok"))
        ids4_ok, ids4_next = sem("ids4_ok"), sem("ids4_next")
        pos_ok, where_ok, slotf_ok, slot_ok = (sem(t) for t in ("pos_ok", "where_ok", "slotf_ok", "slot_ok"))
        ids_out = [sem(f"ids_out{i}") for i in range(2)]
        c_ready, s_tab, tab_ok = sem("c_ready"), sem("s_tab"), sem("tab_ok")
        ids_in = [sem(f"ids_in{i}") for i in range(8)]
        w1_in = [sem(f"w1_in{i}") for i in range(4)]
        w2_in = [sem(f"w2_in{i}") for i in range(4)]
        idc_ok = sem("idc_ok")
        xg_in = [sem(f"xg_in{i}") for i in range(8)]
        stg_ok, mvg_ok, veg_ok, rsg_ok, xgn_ok = (sem(t) for t in ("stg_ok", "mvg_ok", "veg_ok", "rsg_ok", "xgn_ok"))
        gt_ready, gt_evac, h_ready, h_ok, y_ready, og_ok = (
            sem(t) for t in ("gt_ready", "gt_evac", "h_ready", "h_ok", "y_ready", "og_ok"))
        og_out = [sem(f"og_out{i}") for i in range(2)]

        SETUP_DMAS = 20
        x_seq = x.rearrange("(a n) s h -> n s (a h)", a=1)
        ctx_seq = ctx_in.rearrange("(a n) s h -> n s (a h)", a=1)
        bias_seq = bias.rearrange("n h q k -> n q h k")
        x2_seq = x2_dram.rearrange("(n s) h -> n s h", s=P)
        out_rows = out.rearrange("n s h -> (n s) h")

        LOOP = (2, N // U - 1)
        FIRST, LAST = -6, N + 8
        FLOOP = (1, TILES // FU - 1)
        FFIRST, FLAST = -5, TILES + 1

        block = ctx.enter_context(nc.Block())

        def seq(i, k, lag):
            t = At(i, k - lag, U)
            if isinstance(i, int) and not 0 <= i * U + k - lag < N:
                return None
            return t

        def tile(i, k, lag):
            t = At(i, k - lag, FU)
            if isinstance(i, int) and not 0 <= i * FU + k - lag < TILES:
                return None
            return t

        def norms_at(i, k):
            which = [n for n, lag in enumerate((-5, 2)) if seq(i, k, lag)]
            return (which[0], which[-1] + 1) if which else None

        @block.sync
        def _(sp):
            def load(dst, src):
                sp.dma_start(dst, src).then_inc(s_set, 16)

            load(cst[:], consts)
            load(row[:], row_consts)
            load(ids4[:], ids_const)
            for w, wt, a, b in (("q", wqT, aq, bqT), ("k", wkT, ak, bkT), ("v", wvT, av, bvT)):
                load(W[w][:], wt)
                load(A[w][:], a)
                load(B[w][:], b)
            load(bq_col[:], bq)
            load(bk_col[:], bk)
            load(bv_row[:], bv)
            load(bg_all[:], bg.partition_broadcast(P))
            load(wg_sb[:], wg)
            load(g_raw[:, 0:1], g_xattn.partition_broadcast(P))
            load(g_raw[:, 1:2], g_ffn.partition_broadcast(P))
            load(cnt[:], bg)
            sp.wait_ge(s_setg, 1)
            sp.dma_start(list_dram.rearrange("(p c) o -> p (c o)", p=P), empty[:]).then_inc(s_list0, 16)

            sp.wait_ge(s_bv, 4)
            sp.dma_start(bv_rows[:], bv_parts[:].rearrange("o p h -> o (p h)")).then_inc(bv_in, 16)

            def restack(t, part, n, ok, count):
                pair, w = t.k // 2 % 2, "qk"[n]
                sp.wait_ge(ok, count)
                sp.nop(nofuse=True)
                for r, parts in enumerate(PAIRS):
                    if parts[n] == part:
                        sp.dma_start(ST[w][D * r:D * r + D, pair].rearrange("d (h c) t -> d h (c t)", c=KC),
                                     PART[w][:, part, :]).then_inc(qk_in[pair], 16)

            def step(i, k):
                t = seq(i, k, -1)
                if t and t.slot(2) == 0:
                    restack(t, 2, 0, p2_ok, t.per(2, 2, 1))
                    restack(t, 2, 1, p2_ok, t.per(2, 2, 2))
                late = seq(i, k, -2)
                split = late and late.slot(2) == 0
                if split:
                    if late.reached(4):
                        sp.wait_ge(s_ready, late.n(4, -8))
                        sp.nop(nofuse=True)
                    restack(late, 0, 0, p0_ok, late.per(2, 2, 1))
                    restack(late, 0, 1, p0_ok, late.per(2, 2, 2))
                t = seq(i, k, -6)
                if t:
                    if t.reached(4):
                        sp.wait_ge(xt_ready, t.n(1, -3))
                        sp.nop(nofuse=True)
                    sp.dma_start(ctx_sb[:, t.slot(4), :], ctx_seq[t.n()]).then_inc(ctx_inn[t.slot(4)], 16)
                    if t.reached(8):
                        sp.wait_ge(x2_ok, t.n(1, -7))
                        sp.nop(nofuse=True)
                        sp.wait_ge(xn_ok, t.n(1, -7))
                        sp.nop(nofuse=True)
                    sp.dma_start(x_sb[:, t.slot(8), :], x_seq[t.n()]).then_inc(x_in[t.slot(8)], 16)
                if split:
                    restack(late, 1, 0, p1_ok, late.per(2, 2, 1))
                t = seq(i, k, 2)
                if t:
                    sp.wait_ge(x2_ok, t.n(1, 1))
                    sp.nop(nofuse=True)
                    sp.dma_start(x2_seq[t.n()], x2[:, t.slot(2), :]).then_inc(x2_out[t.slot(2)], 16)
                if split:
                    restack(late, 1, 1, p1_ok, late.per(2, 2, 2))
                t = seq(i, k, -3)
                if t:
                    if t.reached(4):
                        sp.wait_ge(tr_ready, t.n(4, -12))
                        sp.nop(nofuse=True)
                    for h in range(0, HEADS, 8):
                        sp.dma_start(sc[:, t.slot(4), h * P:(h + 8) * P].rearrange("p (h k) -> p h k", h=8),
                                     bias_seq[t.n(), :, h:h + 8, :]).then_inc(bias_in[t.slot(4)], 16)

            run_steps(sp, FIRST, LAST, U, LOOP, step)

            for q in x2_out + ids_out:
                sp.wait_ge(q, 16 * (N // 2))
            sp.wait_ge(tab_ok, 1)

            def fstep(i, k):
                t = tile(i, k, -5)
                if t:
                    if t.reached(8):
                        sp.wait_ge(og_out[t.slot(2)], t.per(2, 16 * HALVES, -48 * HALVES))
                        sp.nop(nofuse=True)
                    b = sp.value_load(tile_b[0:1, bass.ds(t.n(), 1)], min_val=0, max_val=LIST - FT)
                    sp.dma_start(ids[:, t.slot(8), :],
                                 list_dram[bass.ds(b, FT), :].rearrange("(p a) o -> p (a o)", p=P)
                                 ).then_inc(ids_in[t.slot(8)], 16)
                t = tile(i, k, -2)
                if t:
                    if t.reached(4):
                        sp.wait_ge(y_ready, t.n(1, -3))
                        sp.nop(nofuse=True)
                    e = sp.value_load(tile_e[0:1, bass.ds(t.n(), 1)], min_val=0, max_val=EXPERTS - 1)
                    sp.dma_start(w1_sb[:, t.slot(4)], w1[e]).then_inc(w1_in[t.slot(4)], 16)
                    sp.dma_start(w2_sb[:, t.slot(4)], w2[e]).then_inc(w2_in[t.slot(4)], 16)
                    sp.dma_start(b2_sb[:, t.slot(4)], b2[bass.ds(e, 1), :]).then_inc(w2_in[t.slot(4)], 16)

            run_steps(sp, FFIRST, FLAST, FU, FLOOP, fstep)
            for q in og_out:
                sp.wait_ge(q, 16 * HALVES * TILES // 2)

        @block.gpsimd
        def _(pool):
            nc.gpsimd.memset(empty[:], NO_TOKEN).then_inc(s_setg, 1)
            nc.gpsimd.memset(V[:], 1.0).then_inc(s_setg, 1)
            pool.wait_ge(s_setd, 10)
            pool.wait_ge(s_list0, 16)

            def subtract_max(t, h):
                pool.wait_ge(max_ok, t.n(2, h + 1))
                s = sc[:, t.slot(4), 1024 * h:1024 * h + 1024].rearrange("p (h k) -> p h k", h=8)
                m = negmax[:, t.slot(2), 8 * h:8 * h + 8].unsqueeze(2).broadcast_to([P, 8, P])
                nc.gpsimd.tensor_tensor(s, s, m, ALU.add).then_inc(sub_ok, 1)

            def rest(t, n):
                w = "qk"[n]
                pool.wait_ge(p0_ok, t.per(2, 2, n + 1))
                if t.reached(2):
                    pool.wait_ge(p2_ok, t.per(2, 2, n - 1))
                nc.gpsimd.tensor_tensor(REST[w][:], F[w][:], PART[w][:, 0, :], ALU.subtract).then_inc(rest_ok, 1)

            def last_part(t, n):
                w = "qk"[n]
                pool.wait_ge(p1_ok, t.per(2, 2, n + 1))
                nc.gpsimd.tensor_tensor(PART[w][:, 2, :], REST[w][:], PART[w][:, 1, :],
                                        ALU.subtract).then_inc(p2_ok, 1)

            def step(i, k):
                cur, late = seq(i, k, 0), seq(i, k, -2)
                split = late and late.slot(2) == 0
                if split:
                    rest(late, 0)
                if cur:
                    subtract_max(cur, 0)
                if split:
                    rest(late, 1)
                if split:
                    last_part(late, 0)
                norms = norms_at(i, k)
                if norms:
                    a, b = norms
                    here = At(i, k, U)
                    pool.wait_ge(ve_ok, here.n(1, 6))
                    if seq(i, k, -4):
                        pool.wait_ge(xn_ok, here.n(1, 5))
                    if seq(i, k, 3):
                        pool.wait_ge(xn2_ok, here.n(1, -2))
                    nc.gpsimd.tensor_tensor(rs[:, a:b, 0], ve[:, a:b, 0], minus_half.broadcast_to([P, b - a]),
                                            ALU.pow).then_inc(rs_ok, 1)
                if split:
                    last_part(late, 1)
                if cur:
                    subtract_max(cur, 1)
                t = seq(i, k, 9)
                if t:
                    pool.wait_ge(slot_ok, t.per(4, 1, 1))
                    pool.nop(nofuse=True)
                    g, j = t.k // 4 % 2, t.slot(4)
                    nc.gpsimd.indirect_dma_start(
                        list_dram, bass.IndirectOffsetOnAxis(ap=slot_i[:, g, j:j + 1], axis=0),
                        ids4_i[:, g, j:j + 1], None).then_inc(ids_out[g], 16)

            run_steps(pool, FIRST, LAST, U, LOOP, step)
            for q in x2_out:
                pool.wait_ge(q, 16 * (N // 2))

            def fstep(i, k):
                t = tile(i, k, -3)
                if t:
                    pool.wait_ge(idc_ok, t.n(1, 1))
                    if t.reached(8):
                        pool.wait_ge(og_ok, t.n(1, -7))
                    pool.nop(nofuse=True)
                    for a in range(HALVES):
                        nc.gpsimd.indirect_dma_start(
                            xg[:, t.slot(8), a, :], None, x2_dram,
                            bass.IndirectOffsetOnAxis(ap=idc[:, t.slot(4), a:a + 1], axis=0)
                        ).then_inc(xg_in[t.slot(8)], 16)
                t = tile(i, k, 2)
                if t:
                    pool.wait_ge(og_ok, t.n(1, 1))
                    pool.nop(nofuse=True)
                    for a in range(HALVES):
                        nc.gpsimd.indirect_dma_start(
                            out_rows, bass.IndirectOffsetOnAxis(ap=ids[:, t.slot(8), a:a + 1], axis=0),
                            og[:, t.slot(2), a, :], None, bounds_check=TOKENS - 1, oob_is_err=False
                        ).then_inc(og_out[t.slot(2)], 16)
                t = tile(i, k, -2)
                if t:
                    pool.wait_ge(veg_ok, t.n(1, 1))
                    nc.gpsimd.tensor_tensor(rsg[:], veg[:], minus_half.broadcast_to([P, HALVES]),
                                            ALU.pow).then_inc(rsg_ok, 1)

            run_steps(pool, FFIRST, FLAST, FU, FLOOP, fstep)

        @block.tensor
        def _(pe):
            mm = nc.tensor.matmul
            pe.wait_ge(s_set, 16 * SETUP_DMAS)
            for n, w in enumerate("qkv"):
                for c in range(KC):
                    ins = mm(bank[n][:, c * HID:(c + 1) * HID], A[w][:, c * P:(c + 1) * P], B[w][:],
                             start=True, stop=True)
            ins.then_inc(s_setp, 1)
            pe.wait_ge(s_setd, 10)

            pe.wait_ge(bv_in, 16)

            def scores(t, q):
                pair, tok = t.k // 2 % 2, P * t.slot(2)
                if q == 0 and t.slot(2) == 0:
                    pe.wait_ge(qk_in[pair], t.per(4, 32 * len(PAIRS), 32 * len(PAIRS)))
                if q >= 2 or t.reached(1):
                    pe.wait_ge(s_used, t.n(4, q - 1))
                for h in range(4 * q, 4 * q + 4):
                    col = h % 8 * KC + h // 8
                    ins = mm(b_s[q % 2][:, P * (h % 4):P * (h % 4) + P], ST["q"][:, pair, col, tok:tok + P],
                             ST["k"][:, pair, col, tok:tok + P], start=True, stop=True)
                ins.then_inc(s_ready, 1)

            def turn(t, q):
                if q % 2 == 0:
                    pe.wait_ge(sub_ok, t.n(2, q // 2 + 1))
                if q >= 2 or t.reached(1):
                    pe.wait_ge(pt_ready, t.n(4, q - 1))
                for h in range(4):
                    o = 512 * q + P * h
                    ins = nc.tensor.transpose(b_t[q % 2][:, P * h:P * h + P], sc[:, t.slot(4), o:o + P], ident)
                ins.then_inc(tr_ready, 1)

            def step(i, k):
                nxt, late, cur, prev, fin, old, gate = (seq(i, k, lag) for lag in (-4, -2, 0, 1, 2, 3, 4))
                here = At(i, k, U)
                if cur:
                    scores(cur, 0)
                if prev:
                    turn(prev, 0)
                if fin:
                    pe.wait_ge(pt_ready, fin.n(4, 4))
                    if fin.reached(1):
                        pe.wait_ge(ot_evac, fin.n())
                    pe.wait_ge(xt_evac, nxt.n() if nxt else N)
                    for h in range(HEADS):
                        j = h % 4
                        ins = mm(b_x[CELL * j:CELL * j + CELL, P * (h // 4):P * (h // 4) + P],
                                 V[:, fin.slot(8), h, :], PT[:, fin.slot(2), P * h:P * h + P],
                                 start=True, stop=True, tile_position=(0, CELL * j))
                    ins.then_inc(ot_ready, 1)
                if late and late.slot(2) == 0:
                    pair = late.k // 2 % 2
                    pe.wait_ge(v_evac, late.n(1, 2))
                    for o in range(KC):
                        for c in range(KC):
                            ins = mm(b_vk[:, 256 * o:256 * o + 256], W["k"][:, c, o * P:o * P + P],
                                     XT[:, pair, KC + c, :], start=(c == 0), stop=(c == KC - 1))
                    ins.then_inc(k_ready, 1)
                if cur:
                    scores(cur, 1)
                if prev:
                    turn(prev, 1)
                if old:
                    pe.wait_ge(xn2_ok, old.n(1, 1))
                    if old.reached(1):
                        pe.wait_ge(x2t_evac, old.n())
                    pe.wait_ge(q_evac, nxt.per(2) if nxt else N // 2)
                    for c in range(KC):
                        ins = nc.tensor.transpose(b_q[:, c * P:c * P + P],
                                                  xn2[:, old.slot(2), c * P:c * P + P], ident)
                    ins.then_inc(x2t_ready, 1)
                ins = None
                if here.reached(3) and (fin or gate or seq(i, k, 5)):
                    pe.wait_ge(o_used, here.n(1, -2))
                if fin:
                    pe.wait_ge(ot_evac, fin.n(1, 1))
                    for g in range(HEADS // 4):
                        ins = nc.tensor.transpose(b_o[:, P * g:P * g + P], OT[:, P * g:P * g + P], ident)
                if gate:
                    pe.wait_ge(x2t_evac, gate.n(1, 1))
                    for c in range(KC):
                        ins = mm(log_ps, x2T[:, gate.slot(2), c, :], wg_sb[:, c, :],
                                 start=(c == 0), stop=(c == KC - 1))
                grp = seq(i, k, 5)
                if grp and grp.slot(4) == 3:
                    pe.wait_ge(cnt_ok, grp.per(4, 4, 4))
                    mm(pos_ps, tri, OH[:], start=True, stop=False)
                    ins = mm(pos_ps, ones, CNT[:, 0:4, :], start=False, stop=True)
                if ins:
                    ins.then_inc(o_ready, 1)
                if nxt:
                    pe.wait_ge(xn_ok, nxt.n(1, 1))
                    pe.wait_ge(ctx_inn[nxt.slot(4)], nxt.per(4, 16, 16))
                    if nxt.reached(1):
                        pe.wait_ge(xt_evac, nxt.n())
                    if fin:
                        pe.wait_ge(ot_evac, fin.n(1, 1))
                    for c in range(KC):
                        nc.tensor.transpose(b_x[:, c * P:c * P + P],
                                            xn[:, nxt.slot(2), c * P:c * P + P], ident)
                    for c in range(KC):
                        ins = nc.tensor.transpose(b_x[:, (KC + c) * P:(KC + c) * P + P],
                                                  ctx_sb[:, nxt.slot(4), c * P:c * P + P], ident)
                    ins.then_inc(xt_ready, 1)
                if cur:
                    scores(cur, 2)
                if prev:
                    turn(prev, 2)
                if nxt:
                    pair, tok = nxt.k // 2 % 2, P * nxt.slot(2)
                    pe.wait_ge(xt_evac, nxt.n(1, 1))
                    if nxt.reached(1):
                        pe.wait_ge(v_evac, nxt.n())
                    if nxt.reached(2):
                        pe.wait_ge(k_evac, nxt.per(2))
                    mm(b_vk[:, 0:HID], ones3[:], bv_rows[:], start=True, stop=False)
                    for c in range(KC):
                        ins = mm(b_vk[:, 0:HID], XT[:, pair, KC + c, tok:tok + P], W["v"][:, c, :],
                                 start=False, stop=(c == KC - 1))
                    ins.then_inc(v_ready, 1)
                if cur:
                    scores(cur, 3)
                if prev:
                    turn(prev, 3)
                if nxt and nxt.slot(2) == 1:
                    if nxt.reached(2):
                        pe.wait_ge(q_evac, nxt.per(2))
                    if old:
                        pe.wait_ge(x2t_evac, old.n(1, 1))
                    for o in range(KC):
                        for c in range(KC):
                            ins = mm(b_q[:, 256 * o:256 * o + 256], W["q"][:, c, o * P:o * P + P],
                                     XT[:, pair, c, :], start=(c == 0), stop=(c == KC - 1))
                    ins.then_inc(q_ready, 1)

            run_steps(pe, FIRST, LAST, U, LOOP, step)

            pe.wait_ge(o_used, N + 3)
            mm(b_o[:, 0:EXPERTS], ones, CNT[:, 4, :], start=True, stop=True).then_inc(c_ready, 1)

            def fstep(i, k):
                t = tile(i, k, 0)
                if t:
                    pe.wait_ge(gt_evac, t.n(1, 1))
                    pe.wait_ge(w1_in[t.slot(4)], t.per(4, 16, 16))
                    if t.reached(2):
                        pe.wait_ge(h_ok, t.n(1, -1))
                    for o in range(KC):
                        for c in range(KC):
                            ins = mm(bank[2 + t.slot(2)][:, FT * o:FT * o + FT],
                                     w1_sb[:, t.slot(4), c * HID + o * P:c * HID + o * P + P],
                                     xgT[:, t.slot(2), c, :], start=(c == 0), stop=(c == KC - 1))
                    ins.then_inc(h_ready, 1)
                t = tile(i, k, -1)
                if t:
                    pe.wait_ge(xgn_ok, t.n(HALVES, HALVES))
                    if t.reached(2):
                        pe.wait_ge(gt_evac, t.n(1, -1))
                    for c in range(KC):
                        for a in range(HALVES):
                            o = c * FT + a * P
                            ins = nc.tensor.transpose(bank[t.slot(2)][:, o:o + P],
                                                      xgn[:, t.slot(2), a, c * P:c * P + P], ident)
                    ins.then_inc(gt_ready, 1)
                t = tile(i, k, 1)
                if t:
                    pe.wait_ge(h_ok, t.n(1, 1))
                    pe.wait_ge(w2_in[t.slot(4)], t.per(4, 32, 32))
                    if t.reached(2):
                        pe.wait_ge(og_ok, t.n(1, -1))
                    for a in range(HALVES):
                        y_half = bank[6 + t.slot(2)][:, HID * a:HID * a + HID]
                        mm(y_half, ones[0:1, :], b2_sb[:, t.slot(4), :], start=True, stop=False)
                        for c in range(KC):
                            ins = mm(y_half, hT[:, t.slot(2), c, a * P:a * P + P],
                                     w2_sb[:, t.slot(4), c * HID:c * HID + HID], start=False, stop=(c == KC - 1))
                    ins.then_inc(y_ready, 1)

            run_steps(pe, FFIRST, FLAST, FU, FLOOP, fstep)

        @block.scalar
        def _(act):
            act.wait_ge(s_set, 16 * SETUP_DMAS)
            nc.scalar.activation(tg[:], g_raw[:], ACT.Tanh).then_inc(s_seta, 1)
            act.wait_ge(s_setd, 10)
            act.wait_ge(s_setg, 2)

            def project(t, n):
                w, ps, ready, evac, col = (("q", b_q, q_ready, q_evac, bq_col),
                                           ("k", b_vk, k_ready, k_evac, bk_col))[n]
                act.wait_ge(ready, t.per(2, 1, 1))
                if t.reached(2):
                    act.wait_ge(rest_ok, t.per(2, 2, n - 1))
                    act.wait_ge(qk_in[(t.k // 2 + 1) % 2], t.minus(2).per(4, 32 * len(PAIRS), 32 * len(PAIRS)))
                for o in range(KC):
                    ins = nc.scalar.activation(F[w][:, 256 * o:256 * o + 256], ps[:, 256 * o:256 * o + 256],
                                               ACT.Identity, bias=col[:, o:o + 1])
                ins.then_inc(evac, 1)
                act.wait_ge(evac, t.per(2, 1, 1))
                nc.scalar.copy(PART[w][:, 0, :], F[w][:]).then_inc(p0_ok, 1)

            def normalise(t, n, at, rows, dst, done, turned):
                act.wait_ge(shift_ok, at)
                if t.reached(2):
                    act.wait_ge(turned, t.n(1, -1))
                nc.scalar.activation(dst[:, t.slot(2), :], rows, ACT.Identity, bias=shift[:, n, :],
                                     scale=rs[:, n, :]).then_inc(done, 1)

            def second_part(t, n):
                w = "qk"[n]
                act.wait_ge(rest_ok, t.per(2, 2, n + 1))
                nc.scalar.copy(PART[w][:, 1, :], REST[w][:]).then_inc(p1_ok, 1)

            def probs(t, q):
                act.wait_ge(tr_ready, t.n(4, q + 1))
                if q == 0 and t.reached(2):
                    act.wait_ge(ot_ready, t.n(1, -1))
                nc.scalar.activation(PT[:, t.slot(2), 512 * q:512 * q + 512], b_t[q % 2][:],
                                     ACT.Exp).then_inc(pt_ready, 1)

            def step(i, k):
                nxt, late, prev, fin, old = (seq(i, k, lag) for lag in (-4, -2, 1, 2, 3))
                split = late and late.slot(2) == 0
                if prev:
                    probs(prev, 0)
                if old:
                    normalise(old, 1, At(i, k, U).n(1, 5), x2[:, old.slot(2), :], xn2, xn2_ok, x2t_ready)
                if fin:
                    act.wait_ge(ot_ready, fin.n(1, 1))
                    if fin.reached(1):
                        act.wait_ge(o_ready, fin.n())
                    nc.scalar.copy(OT[:], b_x[:]).then_inc(ot_evac, 1)
                if nxt:
                    normalise(nxt, 0, At(i, k, U).n(1, 5), x_sb[:, nxt.slot(8), :], xn, xn_ok, xt_ready)
                if split:
                    project(late, 1)
                if prev:
                    probs(prev, 1)
                if old:
                    act.wait_ge(x2t_ready, old.n(1, 1))
                    if old.reached(2):
                        act.wait_ge(o_ready, old.n(1, 1))
                    nc.scalar.copy(x2T[:, old.slot(2)], b_q[:, 0:HID].rearrange("p (c t) -> p c t", t=P)
                                   ).then_inc(x2t_evac, 1)
                if nxt:
                    pair, tok = nxt.k // 2 % 2, P * nxt.slot(2)
                    act.wait_ge(xt_ready, nxt.n(1, 1))
                    if nxt.reached(4):
                        act.wait_ge(k_ready, nxt.per(2, 1, -1))
                    nc.scalar.copy(XT[:, pair, :, tok:tok + P],
                                   b_x[:].rearrange("p (c t) -> p c t", t=P)).then_inc(xt_evac, 1)
                if split:
                    second_part(late, 0)
                if prev:
                    probs(prev, 2)
                if split:
                    second_part(late, 1)
                if nxt:
                    act.wait_ge(v_ready, nxt.n(1, 1))
                    if nxt.reached(8):
                        act.wait_ge(ot_ready, nxt.n(1, -7))
                    nc.scalar.copy(V[:, nxt.slot(8), :, 0:D],
                                   b_vk[:, 0:HID].rearrange("p (h d) -> p h d", d=D)).then_inc(v_evac, 1)
                if prev:
                    probs(prev, 3)
                if nxt and nxt.slot(2) == 1:
                    project(nxt.minus(1), 0)

            run_steps(act, FIRST, LAST, U, LOOP, step)

            def fstep(i, k):
                t = tile(i, k, 0)
                if t:
                    act.wait_ge(h_ready, t.n(1, 1))
                    if t.reached(2):
                        act.wait_ge(y_ready, t.n(1, -1))
                    for o in range(KC):
                        ins = nc.scalar.activation(hT[:, t.slot(2), o, :],
                                                   bank[2 + t.slot(2)][:, FT * o:FT * o + FT], ACT.Gelu,
                                                   bias=w1_sb[:, t.slot(4), KC * HID + o:KC * HID + o + 1])
                    ins.then_inc(h_ok, 1)
                t = tile(i, k, -1)
                if t:
                    act.wait_ge(gt_ready, t.n(1, 1))
                    if t.reached(2):
                        act.wait_ge(h_ready, t.n(1, -1))
                    nc.scalar.copy(xgT[:, t.slot(2)], bank[t.slot(2)][:].rearrange("p (c t) -> p c t", t=FT)
                                   ).then_inc(gt_evac, 1)

            run_steps(act, FFIRST, FLAST, FU, FLOOP, fstep)

        @block.vector
        def _(dve):
            dve.wait_ge(s_set, 16 * SETUP_DMAS)
            dve.wait_ge(s_setp, 1)
            dve.wait_ge(s_seta, 1)
            for n, w in enumerate("qkv"):
                nc.vector.scalar_tensor_tensor(out=W[w][:], in0=bank[n][:].rearrange("p (c h) -> p c h", c=KC),
                                               scalar=LORA, in1=W[w][:], op0=ALU.mult, op1=ALU.add).then_inc(s_setd, 1)
            nc.vector.memset(CNT[:], 0.0).then_inc(s_setd, 1)
            nc.vector.memset(zero8[:], 0.0).then_inc(s_setd, 1)
            dve.wait_ge(s_setd, 5)
            nc.vector.tensor_scalar(W["q"][:], W["q"][:], D ** -0.5, None, ALU.mult).then_inc(s_setd, 1)
            nc.vector.tensor_scalar(bq_col[:], bq_col[:], D ** -0.5, None, ALU.mult).then_inc(s_setd, 1)
            nc.vector.tensor_scalar(W["v"][:], W["v"][:], tg[:, 0:1], None, ALU.mult).then_inc(s_setd, 1)
            nc.vector.tensor_scalar(bv_row[:], bv_row[:], tg[0:1, 0:1], None, ALU.mult).then_inc(s_setd, 1)
            nc.vector.memset(ones3[:], 1.0).then_inc(s_setd, 1)
            dve.wait_ge(s_setd, 10)
            nc.vector.tensor_copy(bv_parts[:, 0, :], bv_row[:]).then_inc(s_bv, 1)
            dve.wait_ge(s_bv, 1)
            nc.vector.tensor_tensor(bv_rest[:], bv_row[:], bv_parts[:, 0, :], ALU.subtract).then_inc(s_bv, 1)
            dve.wait_ge(s_bv, 2)
            nc.vector.tensor_copy(bv_parts[:, 1, :], bv_rest[:]).then_inc(s_bv, 1)
            dve.wait_ge(s_bv, 3)
            nc.vector.tensor_tensor(bv_parts[:, 2, :], bv_rest[:], bv_parts[:, 1, :], ALU.subtract).then_inc(s_bv, 1)

            def row_apply(src, dst, mv, rs, rs_s, done, at, free=None):
                dve.wait_ge(rs_s, at)
                if free:
                    dve.wait_ge(*free)
                nc.vector.tensor_scalar(dst, src, mv[:, 0:1], rs, ALU.subtract, ALU.mult).then_inc(done, 1)

            def add_bias(t, q):
                if q == 0:
                    dve.wait_ge(bias_in[t.slot(4)], t.per(4, 32, 32))
                dve.wait_ge(s_ready, t.n(4, q + 1))
                s = sc[:, t.slot(4), 512 * q:512 * q + 512]
                nc.vector.tensor_tensor(s, b_s[q % 2][:], s, ALU.add).then_inc(s_used, 1)

            def row_max(t, h):
                dve.wait_ge(s_used, t.n(4, 2 * h + 2))
                if h == 0 and t.reached(2):
                    dve.wait_ge(sub_ok, t.n(2, -2))
                nc.vector.tensor_reduce(
                    negmax[:, t.slot(2), 8 * h:8 * h + 8],
                    sc[:, t.slot(4), 1024 * h:1024 * h + 1024].rearrange("p (h k) -> p h k", h=8),
                    AX.X, ALU.max, negate=True).then_inc(max_ok, 1)

            def stats(t, n):
                if t and n == 0:
                    dve.wait_ge(x_in[t.slot(8)], t.per(8, 16, 16))
                    nc.vector.bn_stats(st[:, 0, :], x_sb[:, t.slot(8), :]).then_inc(st_ok[0], 1)
                if t and n == 1:
                    dve.wait_ge(x2_ok, t.n(1, 1))
                    nc.vector.bn_stats(st[:, 1, :], x2[:, t.slot(2), :]).then_inc(st_ok[1], 1)

            def aggregate(t, n):
                if t:
                    dve.wait_ge(st_ok[n], t.n(1, 1))
                    dve.nop(nofuse=True)
                    nc.vector.bn_aggr(mv[:, n, :], st[:, n, :]).then_inc(mv_ok[n], 1)

            def step(i, k):
                cur, done, gate, ahead = seq(i, k, 0), seq(i, k, 2), seq(i, k, 4), seq(i, k, -5)
                here = At(i, k, U)
                if cur:
                    add_bias(cur, 0)
                norms = norms_at(i, k - 1)
                if norms:
                    a, b = norms
                    dve.wait_ge(rs_ok, here.n(1, 5))
                    nc.vector.scalar_tensor_tensor(out=shift[:, a:b, 0], in0=mv[:, a:b, 0], scalar=-1.0,
                                                   in1=rs[:, a:b, 0], op0=ALU.mult, op1=ALU.mult).then_inc(shift_ok, 1)
                if cur:
                    add_bias(cur, 1)
                    row_max(cur, 0)
                if here.reached(2) and (gate or done or seq(i, k, 5)):
                    dve.wait_ge(o_ready, here.n(1, -1))
                    if gate:
                        if gate.slot(4) == 0 and gate.reached(4):
                            dve.wait_ge(oh_ok, gate.per(4))
                        ins = nc.vector.tensor_tensor(L[:, gate.slot(4), :], log_ps, bg_all[:], ALU.add)
                        ins.then_inc(l_ok, 1)
                    grp = seq(i, k, 5)
                    if grp and grp.slot(4) == 3:
                        g = grp.per(4, 1, 1)
                        if grp.reached(7):
                            dve.wait_ge(ids4_next, grp.per(4))
                        ins = nc.vector.tensor_tensor(where[:], pos_ps, ebase, ALU.add)
                        ins.then_inc(pos_ok, 1)
                        dve.wait_ge(pos_ok, g)
                        nc.vector.tensor_tensor(where[:], where[:], OH[:], ALU.mult).then_inc(where_ok, 1)
                        dve.wait_ge(where_ok, g)
                        nc.vector.tensor_reduce(slot_f[:], where[:], AX.X, ALU.add).then_inc(slotf_ok, 1)
                        dve.wait_ge(slotf_ok, g)
                        if grp.reached(11):
                            dve.wait_ge(ids_out[grp.k // 4 % 2], grp.per(8, 64))
                        nc.vector.tensor_copy(ids4_i[:, grp.k // 4 % 2, :], ids4[:]).then_inc(ids4_ok, 1)
                        nc.vector.tensor_copy(slot_i[:, grp.k // 4 % 2, :], slot_f[:]).then_inc(slot_ok, 1)
                        dve.wait_ge(ids4_ok, g)
                        nc.vector.tensor_scalar(ids4[:], ids4[:], float(4 * P), None, ALU.add).then_inc(ids4_next, 1)
                    if done:
                        nc.vector.reciprocal(rden[:], o_ps[:, :, D]).then_inc(rden_ok, 1)
                        stats(ahead, 0)
                        dve.wait_ge(rden_ok, done.n(1, 1))
                        if done.reached(2):
                            dve.wait_ge(x2_out[done.slot(2)], done.per(2, 16))
                            dve.wait_ge(xn2_ok, done.n(1, -1))
                        y = x2[:, done.slot(2), :]
                        nc.vector.tensor_tensor(y.rearrange("p (h d) -> p h d", d=D), o_ps[:, :, 0:D],
                                                rden[:].unsqueeze(2).broadcast_to([P, HEADS, D]),
                                                ALU.mult).then_inc(o_used, 1)
                        aggregate(ahead, 0)
                        dve.wait_ge(o_used, here.n(1, -1))
                        nc.vector.tensor_tensor(y, y, x_sb[:, done.slot(8), :], ALU.add).then_inc(x2_ok, 1)
                    else:
                        if gate:
                            dve.wait_ge(l_ok, gate.n(1, 1))
                        dve.sem_inc(o_used, 1)
                if not done:
                    stats(ahead, 0)
                    aggregate(ahead, 0)
                if cur:
                    add_bias(cur, 2)
                stats(done, 1)
                if cur:
                    add_bias(cur, 3)
                aggregate(done, 1)
                if cur:
                    row_max(cur, 1)
                norms = norms_at(i, k)
                if norms:
                    a, b = norms
                    if ahead:
                        dve.wait_ge(mv_ok[0], ahead.n(1, 1))
                    if done:
                        dve.wait_ge(mv_ok[1], done.n(1, 1))
                    nc.vector.tensor_scalar(ve[:, a:b, 0], mv[:, a:b, 1], EPS, None, ALU.add).then_inc(ve_ok, 1)
                if gate and gate.slot(4) == 3:
                    g = gate.per(4, 1, 1)
                    dve.wait_ge(l_ok, gate.n(1, 1))
                    nc.vector.tensor_reduce(lmax[:], L[:], AX.X, ALU.max).then_inc(lmax_ok, 1)
                    dve.wait_ge(lmax_ok, g)
                    nc.vector.tensor_tensor(key[:], L[:], lmax[:].unsqueeze(2).broadcast_to([P, 4, EXPERTS]),
                                            ALU.is_lt).then_inc(lt_ok, 1)
                    dve.wait_ge(lt_ok, g)
                    nc.vector.scalar_tensor_tensor(out=key[:], in0=key[:], scalar=float(2 * EXPERTS), in1=iota,
                                                   op0=ALU.mult, op1=ALU.add).then_inc(key_ok, 1)
                    dve.wait_ge(key_ok, g)
                    nc.vector.tensor_reduce(pick[:], key[:], AX.X, ALU.min).then_inc(pick_ok, 1)
                    dve.wait_ge(pick_ok, g)
                    nc.vector.tensor_tensor(OH[:], iota, pick[:].unsqueeze(2).broadcast_to([P, 4, EXPERTS]),
                                            ALU.is_equal).then_inc(oh_ok, 1)
                    nc.vector.tensor_copy(CNT[:, 0, :], CNT[:, 4, :]).then_inc(cnt0_ok, 1)
                    dve.wait_ge(oh_ok, g)
                    dve.wait_ge(cnt0_ok, g)
                    for j in range(4):
                        nc.vector.tensor_tensor(CNT[:, j + 1, :], CNT[:, j, :], OH[:, j, :], ALU.add).then_inc(cnt_ok, 1)
                        dve.wait_ge(cnt_ok, gate.per(4, 4, j + 1))

            run_steps(dve, FIRST, LAST, U, LOOP, step)

            made = [0]

            def link(ins):
                made[0] += 1
                ins.then_inc(s_tab, 1)
                dve.wait_ge(s_tab, made[0])

            M = TOKENS // FT
            dve.wait_ge(c_ready, 1)
            link(nc.vector.tensor_copy(cnt[:], b_o[0:1, 0:EXPERTS]))
            link(nc.vector.tensor_tensor(over[:], cnt[:].unsqueeze(2).broadcast_to([1, EXPERTS, M]),
                                         row[:, R_M:R_J].rearrange("p (e m) -> p e m", m=M), ALU.is_gt))
            link(nc.vector.tensor_reduce(nt[:], over[:], AX.X, ALU.add))
            link(nc.vector.tensor_tensor_scan(end[:], nt[:], zero8[:], 0.0, ALU.add, ALU.add))
            link(nc.vector.tensor_tensor(past[:], row[:, R_J:R_J256].rearrange("p (j e) -> p j e", e=EXPERTS),
                                         end[:].unsqueeze(1).broadcast_to([1, TILES, EXPERTS]), ALU.is_ge))
            link(nc.vector.tensor_tensor(ptn[:], past[:], nt[:].unsqueeze(1).broadcast_to([1, TILES, EXPERTS]),
                                         ALU.mult))
            link(nc.vector.tensor_reduce(e_f[:], past[:], AX.X, ALU.add))
            link(nc.vector.tensor_reduce(s_f[:], ptn[:], AX.X, ALU.add))
            link(nc.vector.scalar_tensor_tensor(out=b_f[:], in0=s_f[:], scalar=float(-FT), in1=row[:, R_J256:R_END],
                                                op0=ALU.mult, op1=ALU.add))
            link(nc.vector.scalar_tensor_tensor(out=b_f[:], in0=e_f[:], scalar=float(TOKENS), in1=b_f[:],
                                                op0=ALU.mult, op1=ALU.add))
            link(nc.vector.tensor_scalar(ec_f[:], e_f[:], float(EXPERTS - 1), None, ALU.min))
            link(nc.vector.tensor_copy(tile_e[:], ec_f[:]))
            nc.vector.tensor_copy(tile_b[:], b_f[:]).then_inc(tab_ok, 1)

            def fstep(i, k):
                t = tile(i, k, -1)
                if t:
                    for a in range(HALVES):
                        row_apply(xg[:, t.slot(8), a, :], xgn[:, t.slot(2), a, :], mvg[:, a, :], rsg[:, a:a + 1],
                                  rsg_ok, xgn_ok, t.n(1, 1),
                                  (gt_ready, t.n(1, -1)) if a == 0 and t.reached(2) else None)
                t = tile(i, k, 2)
                if t:
                    dve.wait_ge(y_ready, t.n(1, 1))
                    if t.reached(2):
                        dve.wait_ge(og_out[t.slot(2)], t.per(2, 16 * HALVES))
                    nc.vector.scalar_tensor_tensor(out=og[:, t.slot(2)].rearrange("p a h -> p (a h)"),
                                                   in0=bank[6 + t.slot(2)][:], scalar=tg[:, 1:2],
                                                   in1=xg[:, t.slot(8)].rearrange("p a h -> p (a h)"),
                                                   op0=ALU.mult, op1=ALU.add).then_inc(og_ok, 1)
                t = tile(i, k, -2)
                if t:
                    dve.wait_ge(xg_in[t.slot(8)], t.per(8, 32, 32))
                    for a in range(HALVES):
                        nc.vector.bn_stats(stg[:, a, :], xg[:, t.slot(8), a, :]).then_inc(stg_ok, 1)
                    for a in range(HALVES):
                        dve.wait_ge(stg_ok, t.n(HALVES, a + 1))
                        dve.nop(nofuse=True)
                        nc.vector.bn_aggr(mvg[:, a, :], stg[:, a, :]).then_inc(mvg_ok, 1)
                    dve.wait_ge(mvg_ok, t.n(HALVES, HALVES))
                    nc.vector.tensor_scalar(veg[:], mvg[:, :, 1], EPS, None, ALU.add).then_inc(veg_ok, 1)
                t = tile(i, k, -4)
                if t:
                    dve.wait_ge(ids_in[t.slot(8)], t.per(8, 16, 16))
                    if t.reached(4):
                        dve.wait_ge(xg_in[(t.k + 4) % 8], t.minus(4).per(8, 32, 32))
                    nc.vector.tensor_scalar(idc[:, t.slot(4), :], ids[:, t.slot(8), :], float(TOKENS - 1), None,
                                            ALU.min).then_inc(idc_ok, 1)

            run_steps(dve, FFIRST, FLAST, FU, FLOOP, fstep)


def kernel(**inputs):
    import numpy as np
    import concourse.bacc as bacc
    from concourse.bass_utils import run_bass_kernel_spmd

    a = {k: np.ascontiguousarray(v) for k, v in inputs.items()}

    def chunks(m):
        return np.ascontiguousarray(m.reshape(KC, P, -1).transpose(1, 0, 2))

    arrays = {
        "x": a["x"], "ctx_in": a["ctx_1024"], "bias": a["fside_Bx16xSxS2_0"],
        "g_xattn": a["g_xattn"].reshape(1), "g_ffn": a["g_ffn"].reshape(1),
    }
    def heads_inside(m):
        return np.ascontiguousarray(m.reshape(-1, KC, 8, D).transpose(0, 1, 3, 2).reshape(-1, HID))

    for w in "qkv":
        wt, b, bt = a[f"L0_xattn_W{w}"].T, a[f"L0_xattn_b{w}"], a[f"L0_xattn_B{w}"].T
        if w != "v":
            wt, b, bt = heads_inside(wt), np.ascontiguousarray(heads_inside(b).reshape(KC, P).T), heads_inside(bt)
        b = b.reshape(1, HID) if w == "v" else b
        arrays[f"w{w}T"], arrays[f"b{w}"], arrays[f"b{w}T"] = chunks(wt), b, np.ascontiguousarray(bt)
        arrays[f"a{w}"] = a[f"L0_xattn_A{w}"]
    arrays["wg"] = chunks(a["L0_ffn_Wg"])
    arrays["bg"] = a["L0_ffn_bg"].reshape(1, EXPERTS)
    w1 = np.stack([chunks(m).reshape(P, KC * HID) for m in a["L0_ffn_W1"]])
    b1 = a["L0_ffn_b1"].reshape(EXPERTS, KC, P).transpose(0, 2, 1)
    arrays["w1"] = np.ascontiguousarray(np.concatenate([w1, b1], axis=2))
    arrays["w2"] = np.stack([chunks(m).reshape(P, KC * HID) for m in a["L0_ffn_W2"]])
    arrays["b2"] = a["L0_ffn_b2"]

    c = np.zeros((P, C_END), np.float32)
    c[:, C_ID:C_ID + P] = np.eye(P)
    c[:, C_TRI:C_TRI + P] = np.triu(np.ones((P, P)), 1)
    c[:, C_ONE:C_ONE + P] = 1
    c[:, C_HALF] = -0.5
    c[:, C_IOTA:C_IOTA + 32] = np.tile(np.arange(EXPERTS), 4)
    c[:, C_BASE:C_BASE + 32] = np.tile(np.arange(EXPERTS) * TOKENS, 4)
    r = np.zeros((1, R_END), np.float32)
    r[0, R_M:R_J] = np.tile(np.arange(TOKENS // FT) * FT, EXPERTS)
    r[0, R_J:R_J256] = np.repeat(np.arange(TILES), EXPERTS)
    r[0, R_J256:R_END] = np.arange(TILES) * FT
    arrays["consts"], arrays["row_consts"] = c, r
    arrays["ids_const"] = (np.arange(P)[:, None] + P * np.arange(4)[None, :]).astype(np.float32)

    nc = bacc.Bacc("TRN2", target_bir_lowering=False, num_devices=1)
    order = ["x", "ctx_in", "bias", "g_xattn", "g_ffn", "wqT", "bq", "aq", "bqT", "wkT", "bk", "ak", "bkT",
             "wvT", "bv", "av", "bvT", "wg", "bg", "w1", "w2", "b2", "consts", "row_consts", "ids_const"]
    aps = [nc.dram_tensor(f"in_{n}", arrays[n].shape, mybir.dt.from_np(arrays[n].dtype), kind="ExternalInput").ap()
           for n in order]
    out = nc.dram_tensor("out_0", (N, P, HID), F32, kind="ExternalOutput").ap()
    flamingo_block(nc, *aps, out)
    r = run_bass_kernel_spmd(nc, [{f"in_{n}": arrays[n] for n in order}], core_ids=[0])
    return r.results[0]["out_0"]
```
